# Optimizing a Trainium2 kernel written in Bass

```python
import numpy as np
import jax
import jax.numpy as jnp

def _softmax(x, axis=-1):
    return jax.nn.softmax(x, axis=axis)

def _gelu(x):
    return jax.nn.gelu(x, approximate=True)

def _silu(x):
    return jax.nn.silu(x)

def _sigmoid(x):
    return jax.nn.sigmoid(x)

def _layernorm(x, axis=-1, eps=1e-05):
    m = jnp.mean(x, axis=axis, keepdims=True)
    v = jnp.var(x, axis=axis, keepdims=True)
    return (x - m) / jnp.sqrt(v + eps)

def _scatter_add(tgt, idx, src, axis=0):
    return tgt.at[idx].add(src)

def _segment_sum(src, seg, n):
    return jax.ops.segment_sum(src, seg, n)
kernel_name = 'mk_decoder_preln_d1_seqx_r4_5ba5f8'

def setup_inputs(seed: int=0):
    np.random.seed(seed)
    _w = jnp.asarray

    def _rec_inputs():
        import jax
        import jax.numpy as jnp
        _rk = jax.random.key(seed)
        x = -0.0003929 + 0.9999 * jax.random.normal(jax.random.fold_in(_rk, 1), (4, 1024, 256), jnp.float32)
        _lenS = 1024 - jax.random.randint(jax.random.fold_in(_rk, 7), (4,), 0, max(1, 1024 // 4) + 1, jnp.int32)
        _lenS2 = 77 - jax.random.randint(jax.random.fold_in(_rk, 8), (4,), 0, max(1, 77 // 4) + 1, jnp.int32)
        _ctx_1024P = jax.random.normal(jax.random.fold_in(_rk, 11), (4, 16, 256), jnp.float32)
        _ctx_1024c = jax.random.dirichlet(jax.random.fold_in(_rk, 511), 0.3 * jnp.ones((16,), jnp.float32), (4, 77))
        _ctx_1024t = jnp.einsum('bsk,bkd->bsd', _ctx_1024c, _ctx_1024P)
        _ctx_1024t = _ctx_1024t * jax.lax.rsqrt(jnp.mean(jnp.square(_ctx_1024t)) + 1e-12) * 0.953939
        ctx_1024 = 2.81802e-05 + 1.00001 * (_ctx_1024t + 0.3 * jax.random.normal(jax.random.fold_in(_rk, 611), (4, 77, 256), jnp.float32))
        return (x, ctx_1024)
    x, ctx_1024 = _rec_inputs()

    def _L0_attn_setup():
        import jax, jax.numpy as jnp
        import numpy as np
        B, S, H, HS, BLK = (4, 1024, 16, 256, 64)
        D = HS // H
        key = jax.random.key(seed)
        ks = jax.random.split(key, 7)
        s = np.float32(1.0 / np.sqrt(HS))
        return {'hidden_states': jax.random.normal(ks[0], (B, S, HS), jnp.float32), 'Wq': jax.random.normal(ks[1], (HS, HS), jnp.float32) * s, 'bq': jax.random.normal(ks[2], (HS,), jnp.float32) * s, 'Wk': jax.random.normal(ks[3], (HS, HS), jnp.float32) * s, 'bk': jax.random.normal(ks[4], (HS,), jnp.float32) * s, 'Wv': jax.random.normal(ks[5], (HS, HS), jnp.float32) * s, 'bv': jax.random.normal(ks[6], (HS,), jnp.float32) * s}
    _L0_attn_all = _L0_attn_setup()
    _L0_attn_in = {k: v for k, v in _L0_attn_all.items() if k in ('Wq', 'bq', 'Wk', 'bk', 'Wv', 'bv')}
    del _L0_attn_all

    def _L0_xattn_setup():
        import jax, jax.numpy as jnp
        import numpy as np
        B, L, D = (8, 512, 256)
        key = jax.random.key(seed)
        ks = jax.random.split(key, 9)
        scale = 1.0 / np.sqrt(D)
        return {'query_source': jax.random.normal(ks[0], (B, L, D), dtype=jnp.float32), 'key_source': jax.random.normal(ks[1], (B, L, D), dtype=jnp.float32), 'value_source': jax.random.normal(ks[2], (B, L, D), dtype=jnp.float32), 'Wq': jax.random.normal(ks[3], (D, D), dtype=jnp.float32) * scale, 'bq': jnp.zeros((D,), dtype=jnp.float32), 'Wk': jax.random.normal(ks[4], (D, D), dtype=jnp.float32) * scale, 'bk': jnp.zeros((D,), dtype=jnp.float32), 'Wv': jax.random.normal(ks[5], (D, D), dtype=jnp.float32) * scale, 'bv': jnp.zeros((D,), dtype=jnp.float32)}
    _L0_xattn_all = _L0_xattn_setup()
    _L0_xattn_in = {k: v for k, v in _L0_xattn_all.items() if k in ('Wq', 'bq', 'Wk', 'bk', 'Wv', 'bv')}
    del _L0_xattn_all

    def _L0_ffn_setup():
        import jax, jax.numpy as jnp
        import numpy as np
        from jax import lax
        D_MODEL = 256
        INTER = 256
        N_EXPERTS = 8
        TOP_K = 2
        ROUTE_SCALE = 1.0
        B, S = (2, 1024)
        key = jax.random.key(seed)
        ks = jax.random.split(key, 16)
        sc_d = 1.0 / np.sqrt(D_MODEL)
        sc_f = 1.0 / np.sqrt(INTER)
        inp = {'x': jax.random.normal(ks[0], (B, S, D_MODEL), dtype=jnp.float32), 'gate_w': jax.random.normal(ks[1], (N_EXPERTS, D_MODEL), dtype=jnp.float32) * sc_d, 'w1': jax.random.normal(ks[2], (N_EXPERTS, D_MODEL, INTER), dtype=jnp.float32) * sc_d, 'b1': jnp.zeros((N_EXPERTS, INTER), dtype=jnp.float32), 'w2': jax.random.normal(ks[3], (N_EXPERTS, INTER, D_MODEL), dtype=jnp.float32) * sc_f, 'b2': jnp.zeros((N_EXPERTS, D_MODEL), dtype=jnp.float32), 'w3': jax.random.normal(ks[4], (N_EXPERTS, D_MODEL, INTER), dtype=jnp.float32) * sc_d, 'b3': jnp.zeros((N_EXPERTS, INTER), dtype=jnp.float32), 'sw1': jax.random.normal(ks[5], (D_MODEL, INTER), dtype=jnp.float32) * sc_d, 'sb1': jnp.zeros((INTER,), dtype=jnp.float32), 'sw2': jax.random.normal(ks[6], (INTER, D_MODEL), dtype=jnp.float32) * sc_f, 'sb2': jnp.zeros((D_MODEL,), dtype=jnp.float32), 'sw3': jax.random.normal(ks[7], (D_MODEL, INTER), dtype=jnp.float32) * sc_d, 'sb3': jnp.zeros((INTER,), dtype=jnp.float32)}
        return inp
    _L0_ffn_all = _L0_ffn_setup()
    _L0_ffn_in = {k: v for k, v in _L0_ffn_all.items() if k in ('gate_w', 'w1', 'b1', 'w2', 'b2', 'w3', 'b3', 'sw1', 'sb1', 'sw2', 'sb2', 'sw3', 'sb3')}
    del _L0_ffn_all
    return {'x': x, 'ctx_1024': ctx_1024, 'L0_attn_Wq': _L0_attn_in['Wq'], 'L0_attn_bq': _L0_attn_in['bq'], 'L0_attn_Wk': _L0_attn_in['Wk'], 'L0_attn_bk': _L0_attn_in['bk'], 'L0_attn_Wv': _L0_attn_in['Wv'], 'L0_attn_bv': _L0_attn_in['bv'], 'L0_xattn_Wq': _L0_xattn_in['Wq'], 'L0_xattn_bq': _L0_xattn_in['bq'], 'L0_xattn_Wk': _L0_xattn_in['Wk'], 'L0_xattn_bk': _L0_xattn_in['bk'], 'L0_xattn_Wv': _L0_xattn_in['Wv'], 'L0_xattn_bv': _L0_xattn_in['bv'], 'L0_ffn_gate_w': _L0_ffn_in['gate_w'], 'L0_ffn_w1': _L0_ffn_in['w1'], 'L0_ffn_b1': _L0_ffn_in['b1'], 'L0_ffn_w2': _L0_ffn_in['w2'], 'L0_ffn_b2': _L0_ffn_in['b2'], 'L0_ffn_w3': _L0_ffn_in['w3'], 'L0_ffn_b3': _L0_ffn_in['b3'], 'L0_ffn_sw1': _L0_ffn_in['sw1'], 'L0_ffn_sb1': _L0_ffn_in['sb1'], 'L0_ffn_sw2': _L0_ffn_in['sw2'], 'L0_ffn_sb2': _L0_ffn_in['sb2'], 'L0_ffn_sw3': _L0_ffn_in['sw3'], 'L0_ffn_sb3': _L0_ffn_in['sb3']}

def reference(x, ctx_1024, L0_attn_Wq, L0_attn_bq, L0_attn_Wk, L0_attn_bk, L0_attn_Wv, L0_attn_bv, L0_xattn_Wq, L0_xattn_bq, L0_xattn_Wk, L0_xattn_bk, L0_xattn_Wv, L0_xattn_bv, L0_ffn_gate_w, L0_ffn_w1, L0_ffn_b1, L0_ffn_w2, L0_ffn_b2, L0_ffn_w3, L0_ffn_b3, L0_ffn_sw1, L0_ffn_sb1, L0_ffn_sw2, L0_ffn_sb2, L0_ffn_sw3, L0_ffn_sb3):
    import jax
    import jax.numpy as jnp

    def _L0_attn_ref(hidden_states, Wq, bq, Wk, bk, Wv, bv):
        import jax, jax.numpy as jnp
        import numpy as np
        B, S, H, HS, BLK = (4, 1024, 16, 256, 64)
        D = HS // H
        b, m, _ = hidden_states.shape
        h, d, wm = (H, D, BLK)
        wn = wm
        nb = m // wm
        scale = np.float32(1.0 / np.sqrt(d))

        def heads(x):
            return x.reshape(b, m, h, d).transpose(0, 2, 1, 3)
        q = heads(hidden_states @ Wq.T + bq)
        k = heads(hidden_states @ Wk.T + bk)
        v = heads(hidden_states @ Wv.T + bv)
        qb = q.reshape(b, h, nb, wm, d)
        kb = k.reshape(b, h, nb, wn, d)
        vb = v.reshape(b, h, nb, wn, d)

        def attend(qx, kx, vx):
            scores = jnp.einsum('bhqd,bhkd->bhqk', qx, kx) * scale
            return jnp.einsum('bhqk,bhkd->bhqd', jax.nn.softmax(scores, axis=-1), vx)
        first_ctx = attend(qb[:, :, 0], k, v)[:, :, None]
        k2 = jnp.concatenate([kb[:, :, 0], kb[:, :, 1], kb[:, :, 2], kb[:, :, -1]], axis=2)
        v2 = jnp.concatenate([vb[:, :, 0], vb[:, :, 1], vb[:, :, 2], vb[:, :, -1]], axis=2)
        second_ctx = attend(qb[:, :, 1], k2, v2)[:, :, None]
        exp_k = jnp.concatenate([kb[:, :, 1:-3], kb[:, :, 2:-2], kb[:, :, 3:-1]], axis=3)
        exp_v = jnp.concatenate([vb[:, :, 1:-3], vb[:, :, 2:-2], vb[:, :, 3:-1]], axis=3)
        mq = qb[:, :, 2:-2]
        inner = jnp.einsum('bhlqd,bhlkd->bhlqk', mq, exp_k) * scale
        first_band = jnp.einsum('bhlqd,bhkd->bhlqk', mq, kb[:, :, 0]) * scale
        last_band = jnp.einsum('bhlqd,bhkd->bhlqk', mq, kb[:, :, -1]) * scale
        band = jnp.concatenate([first_band, inner, last_band], axis=-1)
        aw = jax.nn.softmax(band, axis=-1)
        mid_ctx = jnp.einsum('bhlqk,bhlkd->bhlqd', aw[..., wn:4 * wn], exp_v)
        mid_ctx = mid_ctx + jnp.einsum('bhlqk,bhkd->bhlqd', aw[..., :wn], vb[:, :, 0])
        mid_ctx = mid_ctx + jnp.einsum('bhlqk,bhkd->bhlqd', aw[..., -wn:], vb[:, :, -1])
        k3 = jnp.concatenate([kb[:, :, 0], kb[:, :, -3], kb[:, :, -2], kb[:, :, -1]], axis=2)
        v3 = jnp.concatenate([vb[:, :, 0], vb[:, :, -3], vb[:, :, -2], vb[:, :, -1]], axis=2)
        second_last_ctx = attend(qb[:, :, -2], k3, v3)[:, :, None]
        last_ctx = attend(qb[:, :, -1], k, v)[:, :, None]
        ctx = jnp.concatenate([first_ctx, second_ctx, mid_ctx, second_last_ctx, last_ctx], axis=2)
        return ctx.reshape(b, h, m, d).transpose(0, 2, 1, 3).reshape(b, m, h * d)

    def _L0_xattn_ref(query_source, key_source, value_source, Wq, bq, Wk, bk, Wv, bv):
        import jax, jax.numpy as jnp
        import numpy as np
        B, L, D = (8, 512, 256)
        q = query_source @ Wq + bq
        k = key_source @ Wk + bk
        v = value_source @ Wv + bv
        scores = jnp.einsum('bqd,bkd->bqk', q, k)
        attn = jax.nn.softmax(scores, axis=-1)
        out = jnp.einsum('bqk,bkd->bqd', attn, v)
        return out

    def _L0_ffn_ref(x, gate_w, w1, b1, w2, b2, w3, b3, sw1, sb1, sw2, sb2, sw3, sb3):
        import jax, jax.numpy as jnp
        import numpy as np
        from jax import lax
        D_MODEL = 256
        INTER = 256
        N_EXPERTS = 8
        TOP_K = 2
        ROUTE_SCALE = 1.0
        B, S = (2, 1024)
        Bx, Sx, D = x.shape
        xt = x.reshape(-1, D)
        scores = jax.nn.softmax((xt @ gate_w.T).astype(jnp.float32), axis=-1)
        top_vals, top_idx = lax.top_k(scores, TOP_K)
        weights = (top_vals * ROUTE_SCALE).astype(x.dtype)
        combine = jnp.sum(jax.nn.one_hot(top_idx, N_EXPERTS, dtype=x.dtype) * weights[..., None], axis=1)

        def body(acc, p):
            W1, B1, W2, B2, W3, B3, c = p
            h = jax.nn.silu(xt @ W1 + B1) * (xt @ W3 + B3)
            return (acc + c[:, None] * (h @ W2 + B2), None)
        y, _ = lax.scan(body, jnp.zeros_like(xt), (w1, b1, w2, b2, w3, b3, combine.T))
        z = jax.nn.silu(xt @ sw1 + sb1) * (xt @ sw3 + sb3) @ sw2 + sb2
        return (y + z).reshape(Bx, Sx, D)
    x = x + _L0_attn_ref(_layernorm(x, axis=-1), L0_attn_Wq, L0_attn_bq, L0_attn_Wk, L0_attn_bk, L0_attn_Wv, L0_attn_bv)
    x = x + _L0_xattn_ref(_layernorm(x, axis=-1), ctx_1024, ctx_1024, L0_xattn_Wq, L0_xattn_bq, L0_xattn_Wk, L0_xattn_bk, L0_xattn_Wv, L0_xattn_bv)
    x = x + _L0_ffn_ref(_layernorm(x, axis=-1), L0_ffn_gate_w, L0_ffn_w1, L0_ffn_b1, L0_ffn_w2, L0_ffn_b2, L0_ffn_w3, L0_ffn_b3, L0_ffn_sw1, L0_ffn_sb1, L0_ffn_sw2, L0_ffn_sb2, L0_ffn_sw3, L0_ffn_sb3)
    return x

_drawn_inputs = setup_inputs


def setup_inputs(seed=0):
    import zlib

    import numpy as np

    out = dict(_drawn_inputs(seed))
    spreads = {'L0_xattn_bq': (0.0, 0.1),
     'L0_xattn_bk': (0.0, 0.8),
     'L0_xattn_bv': (0.0, 0.1),
     'L0_ffn_b1': (0.0, 0.479),
     'L0_ffn_b2': (0.0, 0.3),
     'L0_ffn_b3': (0.0, 0.489),
     'L0_ffn_sb1': (0.0, 0.1),
     'L0_ffn_sb2': (0.0, 0.1),
     'L0_ffn_sb3': (0.0, 0.1)}
    factors = {'L0_attn_bq': 3.439, 'L0_attn_bk': 8.0}
    for name, (base, spread) in spreads.items():
        noise = np.random.default_rng([zlib.crc32(name.encode()), seed]).standard_normal(out[name].shape)
        drawn = base * np.exp(spread * noise) if base else spread * noise
        out[name] = jnp.asarray(drawn.astype(out[name].dtype))
    for name, factor in factors.items():
        out[name] = (out[name] * factor).astype(out[name].dtype)
    return out
```

```python
import numpy as np
import concourse.bass as bass
from concourse import mybir
from contextlib import ExitStack

BATCH, TOKENS, DIM = 4, 1024, 256
HEADS, HEAD_DIM, BLOCK = 16, 16, 64
KEYS = 77
P = 128
TILES = TOKENS // P
HALF = 4
CHUNKS = DIM // P
HH = HEADS // 2
VW = HEAD_DIM + 1
VPAD = HH * VW + 32 - VW
STEPS = TILES + 1
UNIT_STEPS = 2 * STEPS
EPS = 1e-5
SCALE = HEAD_DIM ** -0.5
SHIFT = 64.0
MAX_SLOTS = HH * STEPS
R0_MAX, R1_MAX = MAX_SLOTS // 2, MAX_SLOTS // 2
R0_FIRST, R0_ROUND = R0_MAX + 1, R0_MAX + 5
R0_BEFORE = R0_FIRST - 2
R1_ROUND = R1_MAX
MAX_PER_STEP = 5
SHIFT_ROW = P - 2
OUT_AT = STEPS + 2
PRIOR_OUT_AT = 2
SHIFT_AT = UNIT_STEPS - 3


ALL_TILES = BATCH * TILES
EXPERTS, TOP_K = 8, 2
GROUP = 2 * P
SHARED_BLOCKS = BATCH * TOKENS // GROUP
BLOCKS = -(-(BATCH * TOKENS * TOP_K // GROUP + EXPERTS - 1) // 4) * 4
LIST_BLOCKS = BATCH * TOKENS // GROUP
ID_COL, GATE_COL = DIM, DIM + 1
ROW = GATE_COL + EXPERTS
NO_TOKEN = 1 << 20
W_SCALE = 16.0
BUFS = 8


def work0_uses(ahead, what):
    at = {"prior_out1": -(-MAX_PER_STEP * (PRIOR_OUT_AT + 1) // 2) + 1, "out0": MAX_PER_STEP * (OUT_AT + 1) // 2 + 3,
          "shift": R0_MAX + 5}
    return at[what] if ahead else {"prior_out1": 1, "out0": 3, "out1": 5}[what]


def need(engine, sem, value):
    if not isinstance(value, int) or value > 0:
        engine.wait_ge(sem, value)


def program(nc, x, wq, wk, wv, bq, bk, bv, ctxT, xwqT, xwk, xwv, xbq, xbk, xbv, gateT, w_all, b1, b3, b2, out):
    f32, f16, i32, u32 = mybir.dt.float32, mybir.dt.float16, mybir.dt.int32, mybir.dt.uint32
    ALU, ACT, AX = mybir.AluOpType, mybir.ActivationFunctionType, mybir.AxisListType
    qk_dram = nc.dram_tensor("qk_parts", [BATCH, 2, 4, P, TOKENS], f16, kind="Internal").ap()
    v_dram = nc.dram_tensor("v_rows", [BATCH, 2, TILES, P, HH * VW], f32, kind="Internal").ap()
    slots = nc.dram_tensor("slots", [BLOCKS * GROUP, ROW], f32, kind="Internal").ap()
    with ExitStack() as ctx:
        def sb(name, shape, dt=f32, scope=ctx):
            return scope.enter_context(nc.sbuf_tensor(name, shape, dt))

        def sem(name):
            return ctx.enter_context(nc.semaphore(name))

        def sems(name, n):
            return [sem(f"{name}{i}") for i in range(n)]

        X = sb("x_rows", [P, BATCH * TILES, DIM])
        ident = sb("ident", [P, P])
        stats = sb("stats", [P, HALF, 6])
        var_eps, halves_neg = sb("var_eps", [P, HALF]), sb("halves_neg", [P, HALF])
        ps = ctx.enter_context(nc.psum_tensor("banks", [P, 8, 512], f32))
        ST = [ps[:, 0:2, :], ps[:, 2:4, :]]
        PO = ps[:, 4:6, :]
        WORK = [ps[:, 6, :], ps[:, 7, :]]

        with ExitStack() as early:
            def sb(name, shape, dt=f32):
                return early.enter_context(nc.sbuf_tensor(name, shape, dt))

            w_sb = [sb(f"w{n}_sb", [P, CHUNKS, DIM]) for n in "qkv"]
            qk_bias = sb("qk_bias", [P, 4])
            bv_all = sb("bv_all", [P, DIM])
            ident16 = sb("ident16", [P, P], f16)
            meanvar = [sb(f"meanvar{i}", [P, HALF, 2]) for i in range(2)]
            rstd = [sb(f"rstd{i}", [P, HALF]) for i in range(2)]
            qk_hi = [sb(f"qk_hi{i}", [P, 4, HALF * P], f16) for i in range(2)]
            qk_lo = [sb(f"qk_lo{i}", [P, 4, HALF * P], f16) for i in range(2)]
            v_out = [sb(f"v_out{i}", [P, HALF, HEADS, VW]) for i in range(2)]
            Kst = [sb(f"k_stack{i}", [P, HH, TOKENS], f16) for i in range(2)]
            Qst = [sb(f"q_stack{i}", [P, HH, TOKENS], f16) for i in range(2)]
            V = [sb(f"v{i}", [P, 3, TILES, VPAD]) for i in range(2)]
            probs = [sb(f"probs{i}", [P, 4, 512]) for i in range(3)]
            xn = [probs[0][:, 2 * i:2 * i + 2, :].rearrange("p a (t d) -> p (a t) d", d=DIM) for i in range(2)]
            xnT = [probs[1][:, 2 * i:2 * i + 2, :] for i in range(2)]
            fills = probs[2][:, 0:2, :].bitcast(f16)
            oT = sb("oT", [P, 2, 512])
            mx = sb("mx", [P, HH, STEPS])
            mm = sb("mm", [P, P], f16)
            mT = [sb(f"mT{i}", [P, P], f16) for i in range(2)]
            rcp = sb("rcp", [P, HALF, 4])
            att = [sb(f"att{i}", [P, HALF, 4, HEAD_DIM]) for i in range(2)]


        def sb(name, shape, dt=f32):
            return ctx.enter_context(nc.sbuf_tensor(name, shape, dt))

        rows = sb("rows", [P, ALL_TILES, ROW])
        mv2, mv3 = sb("mv2", [P, HALF, 2]), sb("mv3", [P, HALF, 2])
        rs2, rs3 = sb("rs2", [P, HALF]), sb("rs3", [P, HALF])
        xn2 = sb("xn2", [P, HALF, DIM])
        xn3 = [sb(f"xn3{i}", [P, HALF, DIM]) for i in range(2)]
        xT2 = [sb(f"xT2{i}", [P, CHUNKS, HALF * P]) for i in range(2)]
        xT3 = sb("xT3", [P, CHUNKS, HALF * P])
        ctx_sb = sb("ctx_sb", [P, CHUNKS, BATCH * KEYS])
        xb_sb = sb("xb_sb", [P, 2 * CHUNKS])
        xbv_all = sb("xbv_all", [KEYS, DIM])
        KcT = sb("KcT", [P, CHUNKS, BATCH * KEYS])
        G = sb("G", [P, CHUNKS, BATCH * KEYS])
        g0 = sb("g0", [1, BATCH * KEYS])
        ones = sb("ones", [1, P])
        Vc = sb("Vc", [KEYS, BATCH, DIM])
        gate_sb = sb("gate_sb", [P, CHUNKS, EXPERTS])
        neg_max, row_sum, row_rec = sb("neg_max", [P, HALF]), sb("row_sum", [P, HALF]), sb("row_rec", [P, HALF])
        cp = sb("cp", [P, HALF, KEYS])
        cpT = sb("cpT", [KEYS, HALF * P])
        logits = sb("logits", [P, ALL_TILES, EXPERTS])
        w_hi = sb("w_hi", [P, EXPERTS + 1, 3, CHUNKS, DIM], f16)
        w_lo = sb("w_lo", [P, EXPERTS + 1, 3, CHUNKS, DIM], f16)
        w_raw = [sb(f"w_raw{i}", [P, 3, CHUNKS, DIM]) for i in range(2)]
        xw = [w_raw[1][:, i, :, :] for i in range(3)]
        b1_sb, b3_sb = sb("b1_sb", [P, EXPERTS + 1, CHUNKS]), sb("b3_sb", [P, EXPERTS + 1, CHUNKS])
        b2_all = sb("b2_all", [P, EXPERTS + 1, DIM])
        token_id = sb("token_id", [P, ALL_TILES], i32)
        blank = sb("blank", [P, ROW])
        e_i, e_f = sb("e_i", [P, EXPERTS], i32), sb("e_f", [P, EXPERTS])
        s_i, s_f = sb("s_i", [P, LIST_BLOCKS], i32), sb("s_f", [P, LIST_BLOCKS])
        blk_i, blk_f = sb("blk_i", [1, BLOCKS], i32), sb("blk_f", [1, BLOCKS])
        before = sb("before", [P, P], f16)
        every = sb("every", [P, P], f16)
        T8 = [P, ALL_TILES, EXPERTS]
        gate_probs, oh, chosen16 = sb("gate_probs", T8), [sb(f"one_hot{i}", T8) for i in range(2)], sb("chosen16", T8, f16)
        t8a, t8b = sb("t8a", T8), sb("t8b", T8)
        t1 = sb("t1", [P, ALL_TILES])
        cnt = [sb(f"cnt{i}", T8) for i in range(2)]
        nb_cmp = sb("nb_cmp", [P, EXPERTS, LIST_BLOCKS])
        nb = [sb(f"nb{i}", [P, EXPERTS]) for i in range(3)]
        list_at = sb("list_at", [P, EXPERTS])
        slot_f, slot = sb("slot_f", [P, TOP_K, ALL_TILES]), sb("slot", [P, TOP_K, ALL_TILES], u32)
        blk_cmp = sb("blk_cmp", [1, BLOCKS, EXPERTS - 1])
        blk_e = sb("blk_e", [1, BLOCKS], i32)
        blk_rows = [sb(f"blk_rows{i}", [P, 2, ROW]) for i in range(BUFS // 2)]
        blk_rows += [w_raw[i // 2][:].rearrange("p a c d -> p (a c d)")[:, 2 * ROW * (i % 2):2 * ROW * (i % 2 + 1)].rearrange("p (t c) -> p t c", t=2)
                     for i in range(BUFS // 2)]
        x_hi, x_lo, h_hi, h_lo = ([xT2[i // 2][:, i % 2, :].bitcast(f16)[:, 512 * j:512 * j + 512].rearrange("p (c t) -> p c t", c=CHUNKS)
                                   for j in range(2)] for i in range(4))
        sil, h_f = ([xn3[i][:, 2 * j:2 * j + 2, :] for j in range(2)] for i in range(2))
        y_sb = [xn2[:, 2 * j:2 * j + 2, :] for j in range(2)]

        eps_added = sem("eps_added")
        fills_ready, filled_in = sem("fills_ready"), sem("filled_in")
        waited_apart = sem("waited_apart")
        consts = sem("consts")
        w_in, x_in = sem("w_in"), sem("x_in")
        ln_step, var_ready, rstd_ready, xn_ready, turned, xT_copied = sem("ln_step"), sem("var_ready"), sem("rstd_ready"), sem("xn_ready"), sems("turned", 2), sem("xT_copied")
        qk_made, hi_made, qk_split = sem("qk_made"), sem("hi_made"), sem("qk_split")
        v_made, v_kept = sems("v_made", 2), sem("v_kept")
        qk_stored, v_stored = sems("qk_stored", 2), sems("v_stored", 2)
        stack_in, v_in, m_in = [sems(f"stack_in{i}_", 2) for i in range(2)], sems("v_in", 2), sems("m_in", 2)
        st_full, exped, pv_done = sems("st_full", 2), sems("exped", 2), sems("pv_done", 3)
        ot_full, rcp_made = sem("ot_full"), sem("rcp_made")
        work_full, work_used = sems("work_full", 2), sems("work_used", 2)
        dve_step, att_free = sem("dve_step"), sems("att_free", 2)
        out_done = sem("out_done")
        late_consts, xw_in = sem("late_consts"), sem("xw_in")
        kc_made, kc_kept, gv_made, gv_kept = sem("kc_made"), sem("kc_kept"), sem("gv_made"), sem("gv_kept")
        stat2, var2, rstd2, xn2_ready, turned2, xT2_copied = (sem(n) for n in ("stat2", "var2", "rstd2", "xn2_ready", "turned2", "xT2_copied"))
        stat3, var3, rstd3, xn3_ready, turned3, xT3_copied = (sem(n) for n in ("stat3", "var3", "rstd3", "xn3_ready", "turned3", "xT3_copied"))
        late_eps, rows_kept = sem("late_eps"), sem("rows_kept")
        cs_made, neg_ready, cp_ready, cp_turned, cpT_copied, cv_made, rec_ready, x2_ready = (
            sem(n) for n in ("cs_made", "neg_ready", "cp_ready", "cp_turned", "cpT_copied", "cv_made", "rec_ready", "x2_ready"))
        lg_made, lg_kept = sem("lg_made"), sem("lg_kept")
        raw_in, scaled, low_made = sems("raw_in", 2), sem("scaled"), sem("low_made")
        ff_bias_in, blank_ready, slots_blank = sem("ff_bias_in"), sem("blank_ready"), sem("slots_blank")
        route, exp_done, ranked, ids_ready, gates_ready = (sem(n) for n in ("route", "exp_done", "ranked", "ids_ready", "gates_ready"))
        dispatched = sem("dispatched")
        rows_in, scattered = sems("blk_rows_in", BUFS), sems("scattered", BUFS)
        x_turned, x_hi_made, x_lo_made = sem("x_turned"), sem("x_hi_made"), sem("x_lo_made")
        a_made, b_made, sil_made, h_made, h_hi_made, h_lo_made = (sem(n) for n in ("a_made", "b_made", "sil_made", "h_made", "h_hi_made", "h_lo_made"))
        y_made, y_read, y_ready, x_added = sem("y_made"), sem("y_read"), sem("y_ready"), sem("x_added")
        base_out = sem("base_out")
        block = ctx.enter_context(nc.Block())

        def x_parts(ap, b, sb_rows):
            base = b * TOKENS
            yield sb_rows[0:64, 0, :], ap[bass.ds(base, 64), :]
            yield sb_rows[64:128, 0, :], ap[bass.ds(base + TOKENS - 64, 64), :]
            yield sb_rows[:, 1:TILES, :], ap[bass.ds(base + 64, TOKENS - P), :].rearrange("(t p) d -> p t d", p=P)

        def halves(eng, before, after):
            before(0, 0)
            with eng.Fori(0, BATCH - 1) as b:
                before(b, 1)
                after(b, 0)
                before(b + 1, 0)
                after(b, 1)
            before(BATCH - 1, 1)
            after(BATCH - 1, 0)
            after(BATCH - 1, 1)

        def rounds(eng, first, unit):
            first()
            unit(0, 0, (0, 1), None)
            with eng.Fori(0, BATCH - 1) as b:
                unit(b, 1, (b + 1, 0), (b, 0))
                unit(b + 1, 0, (b + 1, 1), (b, 1))
            unit(BATCH - 1, 1, None, (BATCH - 1, 0))

        def each_half(eng, step):
            step(0, 0)
            with eng.Fori(0, BATCH - 1) as b:
                step(b, 1, inner=True)
                step(b + 1, 0, inner=True)
            step(BATCH - 1, 1)

        def halves_at(b, s):
            return 2 * b + s

        def wait_apart(engine, sem, value):
            engine.wait_ge(sem, value)
            engine.sem_inc(waited_apart, 1)

        class Block:
            def __init__(self, quad, k):
                self.quad, self.k = quad, k
                self.n = BUFS * quad + k

            def __add__(self, d):
                up, k = divmod(self.k + d, BUFS)
                return Block(self.quad + up, k)

        def each_block(eng, step, count):
            for i in range(3):
                step(Block(0, i), range(count))
            with eng.Fori(0, (count - BUFS) // BUFS) as quad:
                for k in range(3, 3 + BUFS):
                    step(Block(quad, 0) + k, None)
            for i in range(3 + count - BUFS, count + 2):
                step(Block(i // BUFS, i % BUFS), range(count))

        def exists(block, known):
            return known is None or block.n in known

        @block.gpsimd
        def _(pool):
            nc.gpsimd.memset(ident[:], 0.0).then_inc(consts, 1)
            pool.wait_ge(consts, 1)
            nc.gpsimd.affine_select(out=ident[:], in_=ident[:], compare_op=ALU.not_equal, fill=1.0, base=0,
                                    pattern=[[-1, P]], channel_multiplier=1).then_inc(consts, 1)
            pool.wait_ge(consts, 2)
            nc.gpsimd.tensor_copy(ident16[:], ident[:]).then_inc(consts, 1)
            nc.gpsimd.memset(halves_neg[:], -0.5).then_inc(consts, 1)
            filled = 4

            def fill(ap, value):
                nonlocal filled
                pool.wait_ge(consts, filled)
                nc.gpsimd.memset(ap, value).then_inc(consts, 1)
                filled += 1

            for i in range(2):
                fill(v_out[i][:, :, :, HEAD_DIM:VW], 1.0)
            for i in range(2):
                fill(V[i][64:128, 1, :, :], 0.0)
                fill(V[i][0:64, 2, :, :], 0.0)
                fill(V[i][:, 0, :, HH * VW:VPAD], 0.0)
                fill(V[i][0:64, 1, :, HH * VW:VPAD], 0.0)
                fill(V[i][64:128, 2, :, HH * VW:VPAD], 0.0)

            pool.wait_ge(consts, filled)

            def rsqrt(b, s):
                n = 2 * b + s
                wait_apart(pool, var_ready, n + 1)
                nc.gpsimd.tensor_scalar(var_eps[:], meanvar[s][:, :, 1], EPS, None, ALU.add).then_inc(eps_added, 1)
                pool.wait_ge(eps_added, n + 1)
                nc.gpsimd.tensor_tensor(rstd[s][:], var_eps[:], halves_neg[:], ALU.pow).then_inc(rstd_ready, 1)

            with pool.Fori(0, BATCH) as b:
                rsqrt(b, 0)
                rsqrt(b, 1)

            def shift_rows(b, hf, first=None):
                R = 2 * b + hf - 1
                wait_apart(pool, work_used[0], R0_BEFORE + R0_ROUND * R + work0_uses(True, "shift") if first is None else R0_FIRST)
                for part in range(2):
                    pool.dma_start(Qst[hf][SHIFT_ROW + part:SHIFT_ROW + part + 1, :, :].rearrange("o h (t q) -> o (h t) q", q=P),
                                   mT[hf][64 * part:64 * part + 64, :]).then_inc(m_in[hf], 16)

            def add_group(b, hf, g, at):
                for j in range(2):
                    pool.wait_ge(work_used[0], at + j)
                    rows = X[:, bass.ds(b * TILES + HALF * j, HALF), (hf * HH + 4 * g) * HEAD_DIM:(hf * HH + 4 * g + 4) * HEAD_DIM]
                    nc.gpsimd.tensor_tensor(rows, rows, att[j][:].rearrange("p t h d -> p t (h d)"), ALU.add).then_inc(att_free[j], 1)

            def unit(b, hf, ahead, prior):
                before = R0_BEFORE + R0_ROUND * (2 * b + hf)
                if prior:
                    add_group(*prior, 1, before + work0_uses(ahead, "prior_out1"))
                add_group(b, hf, 0, before + work0_uses(ahead, "out0"))
                if ahead:
                    shift_rows(*ahead)
                else:
                    add_group(b, hf, 1, before + work0_uses(ahead, "out1"))

            rounds(pool, lambda: shift_rows(0, 0, first=True), unit)

            for j in range(2):
                pool.wait_ge(att_free[j], 4 * BATCH)

            done = 0

            def made(instruction):
                nonlocal done
                instruction.then_inc(late_consts, 1)
                done += 1
                pool.wait_ge(late_consts, done)

            made(nc.gpsimd.memset(ones[:], 1.0))
            made(nc.gpsimd.memset(every[:], 1.0))
            made(nc.gpsimd.affine_select(out=before[:], in_=every[:], compare_op=ALU.is_gt, fill=0.0, base=0,
                                         pattern=[[1, P]], channel_multiplier=-1))
            made(nc.gpsimd.iota(e_i[:], pattern=[[1, EXPERTS]], base=-EXPERTS, channel_multiplier=0))
            made(nc.gpsimd.tensor_copy(e_f[:], e_i[:]))
            made(nc.gpsimd.iota(s_i[:], pattern=[[GROUP, LIST_BLOCKS]], base=0, channel_multiplier=0))
            made(nc.gpsimd.tensor_copy(s_f[:], s_i[:]))
            made(nc.gpsimd.iota(blk_i[:], pattern=[[1, BLOCKS]], base=0, channel_multiplier=0))
            made(nc.gpsimd.tensor_copy(blk_f[:], blk_i[:]))
            made(nc.gpsimd.iota(token_id[:].rearrange("p (b t) -> p b t", b=BATCH), pattern=[[TOKENS, BATCH], [P, TILES]],
                                base=-BLOCK, channel_multiplier=1))
            first_tiles = token_id[:].rearrange("p (b t) -> p b t", b=BATCH)[:, :, 0]
            made(nc.gpsimd.iota(first_tiles[0:BLOCK], pattern=[[TOKENS, BATCH]], base=0, channel_multiplier=1))
            made(nc.gpsimd.iota(first_tiles[BLOCK:P], pattern=[[TOKENS, BATCH]], base=TOKENS - BLOCK, channel_multiplier=1))
            made(nc.gpsimd.tensor_copy(rows[:, :, ID_COL:ID_COL + 1].bitcast(i32), token_id[:].unsqueeze(2)))
            made(nc.gpsimd.memset(blank[:], 0.0))
            made(nc.gpsimd.memset(blank[:, ID_COL:ID_COL + 1].bitcast(i32), NO_TOKEN))

            def norm_scale(n, turn, var, mv, rs, ready):
                wait_apart(pool, var, n + 1)
                nc.gpsimd.tensor_scalar(var_eps[:], mv[:, :, 1], EPS, None, ALU.add).then_inc(late_eps, 1)
                pool.wait_ge(late_eps, turn + 1)
                nc.gpsimd.tensor_tensor(rs[:], var_eps[:], halves_neg[:], ALU.pow).then_inc(ready, 1)

            def low_part(n, s):
                pool.wait_ge(scaled, n + 1)
                nc.gpsimd.tensor_tensor(w_lo[:, n, :, :, :].rearrange("p a c d -> p (a c d)"), w_raw[s][:].rearrange("p a c d -> p (a c d)"),
                                        w_hi[:, n, :, :, :].rearrange("p a c d -> p (a c d)"), ALU.subtract).then_inc(low_made, 1)

            norm_scale(0, 0, var2, mv2, rs2, rstd2)

            def step(b, s, inner=False):
                n = halves_at(b, s)
                last = not inner and s == 1
                if not last:
                    norm_scale(n + 1, 2 * n + 1, var2, mv2, rs2, rstd2)
                low_part(n, s)
                norm_scale(n, 2 * n + 2 if not last else 2 * n + 1, var3, mv3, rs3, rstd3)
                pool.wait_ge(xn3_ready, n + 1)
                nc.gpsimd.tensor_copy(rows[:, bass.ds(HALF * n, HALF), 0:DIM], xn3[s][:]).then_inc(rows_kept, 1)

            each_half(pool, step)
            low_part(EXPERTS, 0)

            pool.wait_ge(ids_ready, 1)
            pool.wait_ge(gates_ready, 1)
            pool.wait_ge(rows_kept, 2 * BATCH)
            pool.wait_ge(slots_blank, 16 * (BLOCKS // 4))
            for t in range(ALL_TILES):
                for k in range(TOP_K):
                    pool.indirect_dma_start(out=slots, out_offset=bass.IndirectOffsetOnAxis(ap=slot[:, k, t:t + 1], axis=0),
                                            in_=rows[:, t, :], in_offset=None, bounds_check=BLOCKS * GROUP - 1,
                                            oob_is_err=True).then_inc(dispatched, 16)

            def shared_step(i, known):
                if exists(i + -2, known):
                    y = i + -2
                    pool.wait_ge(y_read, y.n + 1)
                    tiles = X[:, bass.ds(2 * y.n, 2), :]
                    nc.gpsimd.tensor_tensor(tiles, tiles, y_sb[y.k % 2][:], ALU.add).then_inc(x_added, 1)

            each_block(pool, shared_step, SHARED_BLOCKS)
            pool.wait_ge(base_out, 48 * BATCH)

            def expert_step(i, known):
                if exists(i + -2, known):
                    y = i + -2
                    wait_apart(pool, y_ready, y.n + 1)
                    prior = y + -1
                    if not isinstance(y.n, int) or y.n > 0:
                        wait_apart(pool, scattered[prior.k], 32 * (prior.quad + 1))
                    for t in range(2):
                        pool.indirect_dma_start(out=out, out_offset=bass.IndirectOffsetOnAxis(
                            ap=blk_rows[y.k][:, t, ID_COL:ID_COL + 1].bitcast(u32), axis=0),
                            in_=y_sb[y.k % 2][:, t, :], in_offset=None, bounds_check=BATCH * TOKENS - 1, oob_is_err=False,
                            compute_op=ALU.add).then_inc(scattered[y.k], 16)

            each_block(pool, expert_step, BLOCKS)
            for k in range(BUFS):
                pool.wait_ge(scattered[k], 32 * (BLOCKS // BUFS))

        @block.sync
        def _(sp):
            for w, dram in zip(w_sb, (wq, wk, wv)):
                sp.dma_start(w[:], dram.rearrange("(c p) n -> p c n", p=P)).then_inc(w_in, 16)
            for i, bias in enumerate((bq, bk)):
                sp.dma_start(qk_bias[:, 2 * i:2 * i + 2], bias.rearrange("(c p) -> p c", p=P), allow_slow_non_contiguous=True).then_inc(w_in, 16)
            sp.dma_start(bv_all[:], bv.partition_broadcast(P)).then_inc(w_in, 16)
            for b in range(BATCH):
                for dst, src in x_parts(x, b, X[:, b * TILES:(b + 1) * TILES, :]):
                    sp.dma_start(dst, src).then_inc(x_in, 16)
                sp.wait_ge(x_in, 48 * (b + 1))
            sp.wait_ge(fills_ready, 2)
            for i in range(2):
                for st in (Kst[i], Qst[i]):
                    sp.dma_start(st[32:SHIFT_ROW, :, :], fills[32:SHIFT_ROW, 0:1, :].broadcast_to([SHIFT_ROW - 32, HH, TOKENS])).then_inc(filled_in, 16)
                sp.dma_start(Kst[i][SHIFT_ROW:P, :, :], fills[SHIFT_ROW:P, 1:2, :].broadcast_to([2, HH, TOKENS])).then_inc(filled_in, 16)

            def store(b, s):
                n = 2 * b + s
                cols = slice(s * 512, s * 512 + 512)
                sp.wait_ge(qk_split, 4 * n + 4)
                for part, src in enumerate((qk_hi[s], qk_lo[s])):
                    sp.dma_start(qk_dram[b, part, :, :, cols].rearrange("i p t -> p i t"),
                                 src[:]).then_inc(qk_stored[s], 16)
                sp.wait_ge(v_kept, 2 * n + 2)
                for hf in range(2):
                    sp.dma_start(v_dram[b, hf, s * HALF:(s + 1) * HALF, :, :].rearrange("t p c -> p t c"),
                                 v_out[s][:, :, hf * HH:(hf + 1) * HH, :].rearrange("p t h c -> p t (h c)")).then_inc(v_stored[s], 16)

            with sp.Fori(0, BATCH) as b:
                store(b, 0)
                store(b, 1)
            for s in range(2):
                sp.wait_ge(qk_stored[s], 32 * BATCH)
                sp.wait_ge(v_stored[s], 32 * BATCH)
            sp.wait_ge(consts, 16)
            sp.wait_ge(filled_in, 96)
            def load_unit(b, hf, again):
                for g in range(2):
                    if again:
                        sp.wait_ge(exped[1], UNIT_STEPS * (2 * b + hf - 2) + STEPS * (g + 1))
                    for dst, which, parts in ((Kst[hf], 1, (0, 0, 1)), (Qst[hf], 0, (1, 0, 0))):
                        for c, part in enumerate(parts):
                            sp.dma_start(dst[16 * c:16 * c + 16, 4 * g:4 * g + 4, :],
                                         qk_dram[b, part, 2 * which + hf, 64 * g:64 * g + 64, :].rearrange("(h d) t -> d h t", d=HEAD_DIM)).then_inc(stack_in[hf][g], 16)
                if again:
                    sp.wait_ge(pv_done[2], UNIT_STEPS // 3 * (2 * b + hf - 1))
                if True:
                    for c, rows in enumerate((slice(0, P), slice(0, 64), slice(64, P))):
                        sp.dma_start(V[hf][rows, c, :, 0:HH * VW], v_dram[b, hf, :, rows, :].rearrange("t p c -> p t c")).then_inc(v_in[hf], 16)

            load_unit(0, 0, False)
            load_unit(0, 1, False)
            with sp.Fori(1, BATCH) as b:
                load_unit(b, 0, True)
                load_unit(b, 1, True)

            for j in range(2):
                sp.wait_ge(att_free[j], 4 * BATCH)

            for w, dram in zip((ctx_sb, *xw, gate_sb), (ctxT, xwqT, xwk, xwv, gateT)):
                sp.dma_start(w[:], dram.rearrange("(c p) n -> p c n", p=P)).then_inc(xw_in, 16)
            for i, bias in enumerate((xbq, xbk)):
                sp.dma_start(xb_sb[:, CHUNKS * i:CHUNKS * i + CHUNKS], bias.rearrange("(c p) -> p c", p=P), allow_slow_non_contiguous=True).then_inc(xw_in, 16)
            sp.dma_start(xbv_all[:], xbv.partition_broadcast(KEYS)).then_inc(xw_in, 16)
            for bias, dram in ((b1_sb, b1), (b3_sb, b3)):
                sp.dma_start(bias[:].rearrange("p e c -> p (e c)"), dram).then_inc(ff_bias_in, 16)
            sp.dma_start(b2_all[:], b2.partition_broadcast(P)).then_inc(ff_bias_in, 16)

            def load_weights(e, s):
                sp.dma_start(w_raw[s][:].rearrange("p a c d -> p (a c) d"), w_all[e, :, :].rearrange("(a p) d -> p a d", p=P)).then_inc(raw_in[s], 16)

            load_weights(0, 0)
            sp.wait_ge(gv_kept, 2)
            load_weights(1, 1)
            sp.wait_ge(late_consts, 15)
            for i in range(BLOCKS // 4):
                rows_of = slots[8 * P * i:8 * P * i + 8 * P, :].rearrange("(t p) c -> p t c", p=P)
                sp.dma_start(rows_of, blank[:].unsqueeze(1).broadcast_to([P, 8, ROW])).then_inc(slots_blank, 16)
            with sp.Fori(0, EXPERTS // 2 - 1) as half:
                for s in range(2):
                    sp.wait_ge(low_made, 2 * half + s + 1)
                    load_weights(2 * half + s + 2, s)
            sp.wait_ge(low_made, EXPERTS - 1)
            load_weights(EXPERTS, 0)

            def load_shared(at):
                sp.dma_start(blk_rows[at.k][:], rows[:, bass.ds(2 * at.n, 2), :]).then_inc(rows_in[at.k], 16)

            sp.wait_ge(rows_kept, 2 * BATCH)
            sp.wait_ge(gates_ready, 1)
            for k in range(BUFS):
                if k == BUFS // 2:
                    sp.wait_ge(low_made, EXPERTS + 1)
                load_shared(Block(0, k))
            with sp.Fori(1, SHARED_BLOCKS // BUFS) as quad:
                for k in range(BUFS):
                    sp.wait_ge(x_turned, BUFS * quad + k - BUFS + 1)
                    load_shared(Block(quad, k))

            def load_expert(at):
                sp.dma_start(blk_rows[at.k][:], slots[bass.ds(GROUP * at.n, GROUP), :].rearrange("(t p) c -> p t c", p=P)).then_inc(rows_in[at.k], 16)

            sp.wait_ge(dispatched, 16 * TOP_K * ALL_TILES)
            for k in range(BUFS):
                sp.wait_ge(x_turned, SHARED_BLOCKS - BUFS + k + 1)
                load_expert(Block(0, k))
            sp.wait_ge(x_added, SHARED_BLOCKS)
            for b in range(BATCH):
                for src, dst in x_parts(out, b, X[:, b * TILES:(b + 1) * TILES, :]):
                    sp.dma_start(dst, src).then_inc(base_out, 16)
            with sp.Fori(1, BLOCKS // BUFS) as quad:
                for k in range(BUFS):
                    sp.wait_ge(scattered[k], 32 * quad)
                    load_expert(Block(quad, k))
            sp.wait_ge(base_out, 48 * BATCH)

        @block.vector
        def _(dve):
            def norm(b, s):
                n = 2 * b + s
                dve.wait_ge(x_in, 48 * (b + 1))
                for t in range(HALF):
                    last = nc.vector.bn_stats(stats[:, t, :], X[:, b * TILES + s * HALF + t, :])
                last.then_inc(ln_step, 1)
                wait_apart(dve, ln_step, n + 1)
                for t in range(HALF):
                    last = nc.vector.bn_aggr(meanvar[s][:, t, :], stats[:, t, :])
                last.then_inc(var_ready, 1)
                dve.wait_ge(rstd_ready, n + 1)
                dve.wait_ge(var_ready, n + 1)
                dve.wait_ge(turned[s], b)
                for t in range(HALF):
                    last = nc.vector.tensor_scalar(xn[s][:, t, :], X[:, b * TILES + s * HALF + t, :], meanvar[s][:, t, 0:1],
                                                   rstd[s][:, t:t + 1], ALU.subtract, ALU.mult)
                last.then_inc(xn_ready, 1)

            nc.vector.memset(fills[:, 0, :], 0.0).then_inc(fills_ready, 1)
            nc.vector.memset(fills[:, 1, :], SHIFT).then_inc(fills_ready, 1)
            dve.wait_ge(consts, 6)
            dve.wait_ge(w_in, 96)

            def split(b, s):
                n = 2 * b + s
                for i in range(4):
                    dve.wait_ge(hi_made, 4 * n + i + 1)
                    if i == 0:
                        dve.wait_ge(qk_stored[s], 32 * b)
                    nc.vector.scalar_tensor_tensor(out=qk_lo[s][:, i, :], in0=ps[:, i, :], scalar=qk_bias[:, i:i + 1],
                                                   in1=qk_hi[s][:, i, :], op0=ALU.add, op1=ALU.subtract).then_inc(qk_split, 1)
                for j in range(2):
                    dve.wait_ge(v_made[s], 2 * b + j + 1)
                    if j == 0:
                        dve.wait_ge(v_stored[s], 32 * b)
                    for t in range(2):
                        last = nc.vector.tensor_tensor(
                            v_out[s][:, 2 * j + t, :, 0:HEAD_DIM],
                            ps[:, 4 + j, 256 * t:256 * t + 256].rearrange("p (h d) -> p h d", d=HEAD_DIM),
                            bv_all[:].rearrange("p (h d) -> p h d", d=HEAD_DIM), ALU.add)
                    last.then_inc(v_kept, 1)

            halves(dve, norm, split)

            class Uses:
                def __init__(self, base):
                    self.base, self.n = base, [0, 0]

                def next(self, r):
                    self.n[r] += 1
                    return self.base[r] + self.n[r]

            def max_slot(uses, i):
                h, j = divmod(i, STEPS)
                r = i % 2
                dve.wait_ge(work_full[r], uses.next(r))
                width = 512 if j < 2 else 320
                col = (0, TILES)[j] if j < 2 else j - 1
                nc.vector.tensor_reduce(mx[:, h, col:col + 1], WORK[r][:, 0:width], AX.X, ALU.max).then_inc(work_used[r], 1)

            def shift(uses, b, hf):
                n = 2 * b + hf
                dve.wait_ge(work_used[0], uses.base[0] + uses.n[0])
                dve.wait_ge(work_used[1], uses.base[1] + uses.n[1])
                nc.vector.tensor_tensor(mx[:, :, 0:1], mx[:, :, 0:1], mx[:, :, TILES:TILES + 1], ALU.max).then_inc(dve_step, 1)
                dve.wait_ge(dve_step, 3 * n + 1)
                hi, lo = (mm[:, 64 * k:64 * k + 64].rearrange("p (h t) -> p h t", t=TILES) for k in range(2))
                nc.vector.tensor_scalar(hi, mx[:, :, 0:TILES], -1.0 / SHIFT, None, ALU.mult).then_inc(dve_step, 1)
                dve.wait_ge(dve_step, 3 * n + 2)
                nc.vector.scalar_tensor_tensor(out=lo, in0=mx[:, :, 0:TILES], scalar=-1.0 / SHIFT, in1=hi,
                                               op0=ALU.mult, op1=ALU.subtract).then_inc(dve_step, 1)
                dve.wait_ge(work_full[0], uses.next(0))
                dve.wait_ge(m_in[hf], 32 * b)
                nc.vector.tensor_copy(mT[hf][:], WORK[0].bitcast(f16)[:, 0:P]).then_inc(work_used[0], 1)

            def normalise(uses, b, hf, g):
                G = 4 * b + 2 * hf + g
                for j in range(2):
                    dve.wait_ge(work_full[0], uses.next(0))
                    o = WORK[0].rearrange("p (t h c) -> p t h c", t=HALF, h=4)
                    nc.vector.reciprocal(rcp[:], o[:, :, :, HEAD_DIM]).then_inc(rcp_made, 1)
                    dve.wait_ge(rcp_made, 2 * G + j + 1)
                    dve.wait_ge(att_free[j], G)
                    nc.vector.tensor_tensor(att[j][:], o[:, :, :, 0:HEAD_DIM],
                                            rcp[:].unsqueeze(3).broadcast_to([P, HALF, 4, HEAD_DIM]), ALU.mult).then_inc(work_used[0], 1)

            def first():
                uses = Uses([0, 0])
                for i in range(MAX_SLOTS):
                    max_slot(uses, i)
                shift(uses, 0, 0)

            def unit(b, hf, ahead, prior):
                R = 2 * b + hf
                uses = Uses([R0_BEFORE + R0_ROUND * R, R1_MAX + R1_ROUND * R])
                if not prior:
                    uses.n[0] = 2
                for q in range(UNIT_STEPS + 1):
                    if ahead:
                        for i in range(MAX_PER_STEP * q, min(MAX_PER_STEP * (q + 1), MAX_SLOTS)):
                            max_slot(uses, i)
                    if q == PRIOR_OUT_AT and prior:
                        normalise(uses, *prior, 1)
                    if q == OUT_AT:
                        normalise(uses, b, hf, 0)
                    if q == SHIFT_AT and ahead:
                        shift(uses, *ahead)
                if not ahead:
                    normalise(uses, b, hf, 1)

            rounds(dve, first, unit)

            for j in range(2):
                dve.wait_ge(att_free[j], 4 * BATCH)

            dve.wait_ge(xw_in, 128)
            dve.wait_ge(gv_made, 3)
            for b in range(BATCH):
                last = nc.vector.tensor_tensor(Vc[:, b, :], ps[0:KEYS, 4 + b // 2, 256 * (b % 2):256 * (b % 2) + 256], xbv_all[:], ALU.add)
            last.then_inc(gv_kept, 1)

            def norm(n, tiles, stat, var, mv, rs, rstd, dst, free, ready):
                for t in range(HALF):
                    last = nc.vector.bn_stats(stats[:, t, :], tiles[t])
                last.then_inc(stat, 1)
                wait_apart(dve, stat, n + 1)
                for t in range(HALF):
                    last = nc.vector.bn_aggr(mv[:, t, :], stats[:, t, :])
                last.then_inc(var, 1)
                dve.wait_ge(rstd, n + 1)
                for s, v in free:
                    dve.wait_ge(s, v)
                for t in range(HALF):
                    last = nc.vector.tensor_scalar(dst[:, t, :], tiles[t], mv[:, t, 0:1], rs[:, t:t + 1], ALU.subtract, ALU.mult)
                last.then_inc(ready, 1)

            def tiles_of(n):
                return [X[:, HALF * n + t, :] for t in range(HALF)]

            norm(0, tiles_of(0), stat2, var2, mv2, rs2, rstd2, xn2, [], xn2_ready)

            def step(b, s, inner=False):
                n = halves_at(b, s)
                last = not inner and s == 1
                dve.wait_ge(cs_made, n + 1)
                nc.vector.tensor_reduce(neg_max[:], ps[:, 0, 0:HALF * KEYS].rearrange("p (t k) -> p t k", k=KEYS), AX.X, ALU.max,
                                        negate=True).then_inc(neg_ready, 1)
                if not last:
                    norm(n + 1, tiles_of(n + 1), stat2, var2, mv2, rs2, rstd2, xn2, [(turned2, n + 1)], xn2_ready)
                dve.wait_ge(cp_ready, n + 1)
                nc.vector.reciprocal(row_rec[:], row_sum[:]).then_inc(rec_ready, 1)
                dve.wait_ge(rec_ready, n + 1)
                dve.wait_ge(cv_made, n + 1)
                for t in range(HALF):
                    tile_ = X[:, HALF * n + t, :]
                    lastx = nc.vector.scalar_tensor_tensor(out=tile_, in0=ps[:, 4 + t // 2, 256 * (t % 2):256 * (t % 2) + 256],
                                                           scalar=row_rec[:, t:t + 1], in1=tile_, op0=ALU.mult, op1=ALU.add)
                lastx.then_inc(x2_ready, 1)
                wait_apart(dve, x2_ready, n + 1)
                norm(n, tiles_of(n), stat3, var3, mv3, rs3, rstd3, xn3[s], [(rows_kept, 2 * b), (turned3, 2 * b)], xn3_ready)
                if isinstance(n, int) and n == 0:
                    return
                keep_logits(n - 1)

            def keep_logits(n):
                dve.wait_ge(lg_made, n + 1)
                nc.vector.tensor_copy(logits[:, bass.ds(HALF * n, HALF), :], ps[:, 0, 320:320 + HALF * EXPERTS].rearrange("p (t e) -> p t e", e=EXPERTS)).then_inc(lg_kept, 1)

            each_half(dve, step)
            keep_logits(2 * BATCH - 1)

            routed = 0

            def link(instruction):
                nonlocal routed
                instruction.then_inc(route, 1)
                routed += 1
                dve.wait_ge(route, routed)

            def per_expert(ap):
                return ap.unsqueeze(2).broadcast_to(T8)

            def per_tile(ap):
                return ap.unsqueeze(1).broadcast_to(T8)

            dve.wait_ge(late_consts, 15)
            dve.wait_ge(lg_kept, 2 * BATCH)
            link(nc.vector.tensor_reduce(t1[:], logits[:], AX.X, ALU.max))
            link(nc.vector.tensor_tensor(logits[:], logits[:], per_expert(t1[:]), ALU.subtract))
            dve.wait_ge(exp_done, 1)
            link(nc.vector.tensor_reduce(t1[:], gate_probs[:], AX.X, ALU.add))
            link(nc.vector.reciprocal(t1[:], t1[:]))
            link(nc.vector.tensor_tensor(gate_probs[:], gate_probs[:], per_expert(t1[:]), ALU.mult))
            left = gate_probs
            for k in range(TOP_K):
                link(nc.vector.tensor_reduce(t1[:], left[:], AX.X, ALU.max))
                link(nc.vector.tensor_tensor(t8b[:], left[:], per_expert(t1[:]), ALU.is_equal))
                link(nc.vector.tensor_tensor(t8b[:], t8b[:], per_tile(e_f[:]), ALU.mult))
                link(nc.vector.tensor_reduce(t1[:], t8b[:], AX.X, ALU.min))
                link(nc.vector.tensor_tensor(oh[k][:], per_tile(e_f[:]), per_expert(t1[:]), ALU.is_equal))
                if k == 0:
                    link(nc.vector.scalar_tensor_tensor(out=t8a[:], in0=oh[0][:], scalar=-2.0, in1=gate_probs[:], op0=ALU.mult, op1=ALU.add))
                    left = t8a
            link(nc.vector.tensor_tensor(t8b[:], oh[0][:], oh[1][:], ALU.add))
            link(nc.vector.tensor_copy(chosen16[:], t8b[:]))
            nc.vector.scalar_tensor_tensor(out=rows[:, :, GATE_COL:GATE_COL + EXPERTS], in0=t8b[:], scalar=W_SCALE ** -2,
                                           in1=gate_probs[:], op0=ALU.mult, op1=ALU.mult).then_inc(gates_ready, 1)
            dve.wait_ge(ranked, 1)
            link(nc.vector.tensor_copy(cnt[0][:], ps[:, 2, 0:ALL_TILES * EXPERTS].rearrange("p (t e) -> p t e", e=EXPERTS)))
            src, step_ = 0, 1
            while step_ < ALL_TILES:
                nc.vector.tensor_copy(cnt[1 - src][:, 0:step_, :], cnt[src][:, 0:step_, :])
                link(nc.vector.tensor_tensor(cnt[1 - src][:, step_:, :], cnt[src][:, step_:, :], cnt[src][:, 0:ALL_TILES - step_, :], ALU.add))
                src, step_ = 1 - src, 2 * step_
            totals = cnt[src][:, ALL_TILES - 1, :]
            link(nc.vector.tensor_tensor(nb_cmp[:], totals.unsqueeze(2).broadcast_to([P, EXPERTS, LIST_BLOCKS]),
                                         s_f[:].unsqueeze(1).broadcast_to([P, EXPERTS, LIST_BLOCKS]), ALU.is_gt))
            link(nc.vector.tensor_reduce(nb[0][:], nb_cmp[:], AX.X, ALU.add))
            link(nc.vector.tensor_copy(nb[2][:], nb[0][:]))
            at, d = 0, 1
            while d < EXPERTS:
                nc.vector.tensor_copy(nb[1 - at][:, 0:d], nb[at][:, 0:d])
                link(nc.vector.tensor_tensor(nb[1 - at][:, d:], nb[at][:, d:], nb[at][:, 0:EXPERTS - d], ALU.add))
                at, d = 1 - at, 2 * d
            ends = nb[at]
            link(nc.vector.tensor_tensor(list_at[:], ends[:], nb[2][:], ALU.subtract))
            link(nc.vector.tensor_scalar(list_at[:], list_at[:], float(GROUP), None, ALU.mult))
            link(nc.vector.tensor_tensor(t8a[:], cnt[src][:], ps[:, 1, 0:ALL_TILES * EXPERTS].rearrange("p (t e) -> p t e", e=EXPERTS), ALU.add))
            link(nc.vector.tensor_tensor(cnt[1 - src][:], per_tile(list_at[:]),
                                         ps[:, 2, 0:ALL_TILES * EXPERTS].rearrange("p (t e) -> p t e", e=EXPERTS), ALU.subtract))
            link(nc.vector.tensor_tensor(t8a[:], t8a[:], cnt[1 - src][:], ALU.add))
            for k in range(TOP_K):
                link(nc.vector.tensor_tensor(t8b[:], t8a[:], oh[k][:], ALU.mult))
                link(nc.vector.tensor_reduce(slot_f[:, k, :], t8b[:], AX.X, ALU.add))
            nc.vector.tensor_copy(slot[:], slot_f[:]).then_inc(ids_ready, 1)
            link(nc.vector.tensor_tensor(blk_cmp[:], blk_f[:].unsqueeze(2).broadcast_to([1, BLOCKS, EXPERTS - 1]),
                                         ends[0:1, 0:EXPERTS - 1].unsqueeze(1).broadcast_to([1, BLOCKS, EXPERTS - 1]), ALU.is_ge))
            link(nc.vector.tensor_reduce(blk_f[:], blk_cmp[:], AX.X, ALU.add))
            nc.vector.tensor_copy(blk_e[:], blk_f[:]).then_inc(ids_ready, 1)
            dve.wait_ge(ff_bias_in, 48)
            nc.vector.tensor_scalar(b3_sb[:], b3_sb[:], W_SCALE, None, ALU.mult)
            link(nc.vector.tensor_scalar(b2_all[:, 0:EXPERTS, :], b2_all[:, 0:EXPERTS, :], W_SCALE ** 2, None, ALU.mult))

            def ff_step(shared, first):
                def step(i, known):
                    a = i + -1
                    if exists(a, known):
                        n = first + a.n
                        e = EXPERTS if shared else dve.value_load(blk_e[0:1, bass.ds(a.n, 1)], min_val=0, max_val=EXPERTS - 1)
                        dve.wait_ge(sil_made, n + 1)
                        dve.wait_ge(b_made, n + 1)
                        need(dve, h_hi_made, n - 1)
                        for m in range(CHUNKS):
                            last = nc.vector.scalar_tensor_tensor(out=h_f[a.k % 2][:, m, :], in0=ps[:, 4 + a.k % 2, GROUP * m:GROUP * m + GROUP],
                                                                  scalar=b3_sb[:, e, m:m + 1], in1=sil[a.k % 2][:, m, :], op0=ALU.add, op1=ALU.mult)
                        last.then_inc(h_made, 1)
                    t = i + 1
                    if exists(t, known):
                        split_x(t, first)
                    if exists(a, known):
                        n = first + a.n
                        dve.wait_ge(h_hi_made, n + 1)
                        nc.vector.tensor_tensor(h_lo[a.k % 2][:], h_f[a.k % 2][:], h_hi[a.k % 2][:], ALU.subtract).then_inc(h_lo_made, 1)
                    y = i + -2
                    if shared:
                        if exists(y, known):
                            n = first + y.n
                            dve.wait_ge(y_made, n + 1)
                            need(dve, x_added, n - 1)
                            nc.vector.scalar_tensor_tensor(out=y_sb[y.k % 2][:], in0=ps[:, 6 + y.k % 2, :].rearrange("p (t d) -> p t d", t=2), scalar=W_SCALE ** -2,
                                                           in1=b2_all[:, EXPERTS:EXPERTS + 1, :].broadcast_to([P, 2, DIM]),
                                                           op0=ALU.mult, op1=ALU.add).then_inc(y_read, 1)
                    else:
                        if exists(y, known):
                            e = dve.value_load(blk_e[0:1, bass.ds(y.n, 1)], min_val=0, max_val=EXPERTS - 1)
                            dve.wait_ge(y_read, first + y.n + 1)
                            for t_ in range(2):
                                last = nc.vector.scalar_tensor_tensor(out=y_sb[y.k % 2][:, t_, :], in0=b2_all[:, e, :],
                                                                      scalar=blk_rows[y.k][:, t_, bass.ds(GATE_COL + e, 1)],
                                                                      in1=y_sb[y.k % 2][:, t_, :], op0=ALU.mult, op1=ALU.add)
                            last.then_inc(y_ready, 1)
                return step

            def split_x(t, first):
                n = first + t.n
                dve.wait_ge(x_hi_made, n + 1)
                nc.vector.tensor_tensor(x_lo[t.k % 2][:].rearrange("p c t -> p (c t)"), ps[:, t.k % 2, :],
                                        x_hi[t.k % 2][:].rearrange("p c t -> p (c t)"), ALU.subtract).then_inc(x_lo_made, 1)

            split_x(Block(0, 0), 0)
            each_block(dve, ff_step(True, 0), SHARED_BLOCKS)
            split_x(Block(0, 0), SHARED_BLOCKS)
            each_block(dve, ff_step(False, SHARED_BLOCKS), BLOCKS)

        @block.scalar
        def _(act):
            act.wait_ge(w_in, 96)

            def copy_xT(b, s):
                n = 2 * b + s
                act.wait_ge(turned[s], b + 1)
                act.wait_ge(v_made[s], 2 * b)
                for c in range(CHUNKS):
                    last = nc.scalar.copy(xnT[s][:, c, :], ps[:, 6 + c, :])
                last.then_inc(xT_copied, 1)

            def keep_hi(b, s):
                n = 2 * b + s
                act.wait_ge(qk_stored[s], 32 * b)
                for i in range(4):
                    act.wait_ge(qk_made, 4 * n + i + 1)
                    nc.scalar.activation(qk_hi[s][:, i, :], ps[:, i, :], ACT.Identity,
                                         bias=qk_bias[:, i:i + 1]).then_inc(hi_made, 1)

            halves(act, copy_xT, keep_hi)

            def copy_out(b, hf, g):
                G = 4 * b + 2 * hf + g
                act.wait_ge(pv_done[2], UNIT_STEPS // 3 * (2 * b + hf) + (STEPS // 3) * (g + 1))
                nc.scalar.copy(oT[:], PO).then_inc(ot_full, 1)

            def unit(b, hf, ahead, prior):
                R = 2 * b + hf
                for q in range(UNIT_STEPS):
                    width = 512 if q % STEPS < 2 else 320
                    for p in range(2):
                        act.wait_ge(st_full[p], UNIT_STEPS * R + q + 1)
                        if p == 0:
                            act.wait_ge(pv_done[q % 3], UNIT_STEPS // 3 * R + q // 3)
                        nc.scalar.activation(probs[q % 3][:, 2 * p:2 * p + 2, 0:width], ST[p][:, :, 0:width],
                                             ACT.Exp, scale=SCALE).then_inc(exped[p], 1)
                    if q == 0 and prior:
                        copy_out(*prior, 1)
                    if q == STEPS:
                        copy_out(b, hf, 0)
                if not ahead:
                    copy_out(b, hf, 1)

            rounds(act, lambda: None, unit)

            for j in range(2):
                act.wait_ge(att_free[j], 4 * BATCH)

            act.wait_ge(xw_in, 128)
            for m in range(CHUNKS):
                act.wait_ge(kc_made, m + 1)
                nc.scalar.activation(KcT[:, m, :], ps[:, m, 0:BATCH * KEYS], ACT.Identity, bias=xb_sb[:, CHUNKS + m:CHUNKS + m + 1]).then_inc(kc_kept, 1)
            act.wait_ge(gv_made, 3)
            for m in range(CHUNKS):
                nc.scalar.copy(G[:, m, :], ps[:, 2 + m, 0:BATCH * KEYS])
            nc.scalar.copy(g0[:], ps[0:1, 6, 0:BATCH * KEYS]).then_inc(gv_kept, 1)

            def copy_xT(n, s, turned, base, dst, free, ready):
                act.wait_ge(turned, n + 1)
                for sm, v in free:
                    act.wait_ge(sm, v)
                for c in range(CHUNKS):
                    last = nc.scalar.copy(dst[:, c, :], ps[:, base + c, :])
                last.then_inc(ready, 1)

            def split_weights(n, s, times):
                act.wait_ge(raw_in[s], 16 * times)
                flat = w_raw[s][:].rearrange("p a c d -> p (a c d)")
                nc.scalar.mul(w_hi[:, n, :, :, :].rearrange("p a c d -> p (a c d)"), flat, W_SCALE)
                nc.scalar.mul(flat, flat, W_SCALE).then_inc(scaled, 1)

            copy_xT(0, 0, turned2, 1, xT2[0], [], xT2_copied)

            def step(b, s, inner=False):
                n = halves_at(b, s)
                first, last = not inner and s == 0, not inner and s == 1
                act.wait_ge(neg_ready, n + 1)
                for t in range(HALF):
                    lastp = nc.scalar.activation(cp[:, t, :], ps[:, 0, KEYS * t:KEYS * t + KEYS], ACT.Exp, bias=neg_max[:, t:t + 1],
                                                 accum_out=row_sum[:, t:t + 1])
                lastp.then_inc(cp_ready, 1)
                if not last:
                    copy_xT(n + 1, 1 - s, turned2, 1, xT2[1 - s], [], xT2_copied)
                act.wait_ge(cp_turned, n + 1)
                nc.scalar.copy(cpT[:], ps[0:KEYS, 3, :]).then_inc(cpT_copied, 1)
                if not first:
                    copy_xT(n - 1, 1 - s, turned3, 6, xT3, [], xT3_copied)
                split_weights(n, s, b + 1)

            each_half(act, step)
            copy_xT(2 * BATCH - 1, 1, turned3, 6, xT3, [], xT3_copied)
            split_weights(EXPERTS, 0, EXPERTS // 2 + 1)
            act.wait_ge(route, 2)
            nc.scalar.activation(gate_probs[:], logits[:], ACT.Exp).then_inc(exp_done, 1)
            act.wait_ge(ff_bias_in, 48)

            def high_x(t, first):
                n = first + t.n
                act.wait_ge(x_turned, n + 1)
                need(act, b_made, n - 1)
                nc.scalar.copy(x_hi[t.k % 2][:].rearrange("p c t -> p (c t)"), ps[:, t.k % 2, :]).then_inc(x_hi_made, 1)

            def ff_step(shared, first):
                def step(i, known):
                    a = i + -1
                    if exists(a, known):
                        n = first + a.n
                        e = EXPERTS if shared else act.value_load(blk_e[0:1, bass.ds(a.n, 1)], min_val=0, max_val=EXPERTS - 1)
                        act.wait_ge(a_made, n + 1)
                        need(act, h_made, n - 1)
                        for m in range(CHUNKS):
                            last = nc.scalar.activation(sil[a.k % 2][:, m, :], ps[:, 2 + a.k % 2, GROUP * m:GROUP * m + GROUP], ACT.Silu,
                                                        bias=b1_sb[:, e, m:m + 1], scale=1.0 / W_SCALE)
                        last.then_inc(sil_made, 1)
                    t = i + 1
                    if exists(t, known):
                        high_x(t, first)
                    if exists(a, known):
                        n = first + a.n
                        act.wait_ge(h_made, n + 1)
                        need(act, y_made, n - 1)
                        nc.scalar.copy(h_hi[a.k % 2][:], h_f[a.k % 2][:]).then_inc(h_hi_made, 1)
                    y = i + -2
                    if not shared and exists(y, known):
                        e = act.value_load(blk_e[0:1, bass.ds(y.n, 1)], min_val=0, max_val=EXPERTS - 1)
                        act.wait_ge(y_made, first + y.n + 1)
                        prior = y + -2
                        need(act, scattered[prior.k], 32 * (prior.quad + 1))
                        for t_ in range(2):
                            last = nc.scalar.activation(y_sb[y.k % 2][:, t_, :], ps[:, 6 + y.k % 2, DIM * t_:DIM * t_ + DIM], ACT.Copy,
                                                        scale=blk_rows[y.k][:, t_, bass.ds(GATE_COL + e, 1)])
                        last.then_inc(y_read, 1)
                return step

            high_x(Block(0, 0), 0)
            each_block(act, ff_step(True, 0), SHARED_BLOCKS)
            act.wait_ge(ids_ready, 2)
            act.wait_ge(x_added, SHARED_BLOCKS)
            high_x(Block(0, 0), SHARED_BLOCKS)
            each_block(act, ff_step(False, SHARED_BLOCKS), BLOCKS)

        @block.tensor
        def _(pe):
            pe.wait_ge(consts, 3)
            pe.wait_ge(w_in, 96)

            def turn(b, s):
                n = 2 * b + s
                pe.wait_ge(xn_ready, n + 1)
                pe.wait_ge(xT_copied, n)
                for c in range(CHUNKS):
                    for t in range(HALF):
                        last = nc.tensor.transpose(ps[:, 6 + c, P * t:P * t + P], xn[s][:, t, P * c:P * c + P], ident[:])
                last.then_inc(turned[s], 1)

            def project(b, s):
                n = 2 * b + s
                pe.wait_ge(xT_copied, n + 1)
                pe.wait_ge(qk_split, 4 * n)
                for i in range(4):
                    for c in range(CHUNKS):
                        last = nc.tensor.matmul(ps[:, i, :], w_sb[i // 2][:, c, P * (i % 2):P * (i % 2) + P], xnT[s][:, c, :],
                                                start=(c == 0), stop=(c == CHUNKS - 1))
                    last.then_inc(qk_made, 1)
                pe.wait_ge(v_kept, 2 * n)
                for t in range(HALF):
                    for c in range(CHUNKS):
                        last = nc.tensor.matmul(ps[:, 4 + t // 2, 256 * (t % 2):256 * (t % 2) + 256],
                                                xnT[s][:, c, P * t:P * t + P], w_sb[2][:, c, :],
                                                start=(c == 0), stop=(c == CHUNKS - 1))
                    if t % 2:
                        last.then_inc(v_made[s], 1)

            halves(pe, turn, project)
            pe.wait_ge(qk_split, 8 * BATCH)
            pe.wait_ge(v_kept, 4 * BATCH)
            pe.wait_ge(xT_copied, 2 * BATCH)

            class Uses:
                def __init__(self, base):
                    self.base, self.n = base, [0, 0]

                def next(self, r):
                    self.n[r] += 1
                    return self.base[r] + self.n[r] - 1

            def max_slot(uses, i, hf):
                h, j = divmod(i, STEPS)
                r = i % 2
                K, Q, W = Kst[hf][0:SHIFT_ROW, h, :], Qst[hf][0:SHIFT_ROW, h, :], WORK[r]
                pe.wait_ge(work_used[r], uses.next(r))
                if j < 2:
                    last = nc.tensor.matmul(W, Q[:, 0:P], K[:, 512 * j:512 * j + 512], start=True, stop=True)
                else:
                    t = j - 1
                    nc.tensor.matmul(W[:, 0:P], Q[:, P * t:P * t + P], K[:, 0:P], start=True, stop=True)
                    nc.tensor.matmul(W[0:64, P:320], Q[:, P * t:P * t + 64], K[:, P * t - 64:P * t + P], start=True, stop=True)
                    if t < TILES - 1:
                        last = nc.tensor.matmul(W[64:128, P:320], Q[:, P * t + 64:P * t + P], K[:, P * t:P * t + 192], start=True, stop=True)
                    else:
                        nc.tensor.matmul(W[64:128, P:256], Q[:, P * t + 64:P * t + P], K[:, P * t:P * t + P], start=True, stop=True)
                        last = nc.tensor.matmul(W[64:128, 256:320], Q[:, P * t + 64:P * t + P], K[:, P * t:P * t + 64], start=True, stop=True)
                last.then_inc(work_full[r], 1)

            def shift(uses, b, hf):
                pe.wait_ge(dve_step, 3 * (2 * b + hf) + 3)
                pe.wait_ge(work_used[0], uses.next(0))
                nc.tensor.transpose(WORK[0].bitcast(f16)[:, 0:P], mm[:], ident16[:]).then_inc(work_full[0], 1)

            def scores(b, hf, q, p):
                R = 2 * b + hf
                g, step = divmod(q, STEPS)
                if True:
                    pe.wait_ge(exped[p], UNIT_STEPS * R + q)
                    for k in range(2):
                        h = 4 * g + 2 * p + k
                        K, Q, S = Kst[hf][:, h, :], Qst[hf][:, h, :], ST[p][:, k, :]
                        if step < 2:
                            last = nc.tensor.matmul(S, K[:, 0:P], Q[:, 512 * step:512 * step + 512], start=True, stop=True)
                        else:
                            t = step - 1
                            nc.tensor.matmul(S[:, 0:256].rearrange("p (a q) -> p a q", a=2), K[:, P * t:P * t + P],
                                             Q.rearrange("p (a q) -> p a q", q=P)[:, 0:t + 1:t, :], start=True, stop=True)
                            before = Q[:, P * t - 64:P * t]
                            after = Q[:, P * t + P:P * t + 192] if t < TILES - 1 else None
                            if t == 1:
                                last = nc.tensor.matmul(S[:, 256:320], K[:, P * t:P * t + P], after, start=True, stop=True)
                            elif t == TILES - 1:
                                last = nc.tensor.matmul(S[:, 256:320], K[:, P * t:P * t + P], before, start=True, stop=True)
                            else:
                                nc.tensor.matmul(S[0:64, 256:320], K[:, P * t:P * t + 64], before, start=True, stop=True)
                                last = nc.tensor.matmul(S[64:128, 256:320], K[:, P * t + 64:P * t + P], after, start=True, stop=True)
                    last.then_inc(st_full[p], 1)

            def values(b, hf, q):
                R = 2 * b + hf
                g, step = divmod(q, STEPS)
                if q == 0:
                    pe.wait_ge(v_in[hf], 48 * (b + 1))
                if step == 0:
                    pe.wait_ge(ot_full, 2 * R + g)
                for p in range(2):
                    pe.wait_ge(exped[p], UNIT_STEPS * R + q + 1)
                pr = probs[q % 3]
                key_tile = max(step - 1, 0)

                def add(which, cols, tokens, start=False, stop=False):
                    for k in range(4):
                        bank, at = divmod(tokens.start, 512)
                        h = 4 * g + k
                        last = nc.tensor.matmul(PO[32 * k:32 * k + 32, bank, at:at + tokens.stop - tokens.start],
                                                V[hf][:, which, key_tile, h * VW:h * VW + 32],
                                                pr[:, k, cols], start=start, stop=stop, skip_group_check=True)
                    return last

                if step < 2:
                    for half in range(2):
                        last = add(0, slice(256 * half, 256 * half + 256), slice(512 * step + 256 * half, 512 * step + 256 * half + 256), start=half == 0)
                        if half == 0:
                            yield
                else:
                    t = key_tile
                    last = add(0, slice(0, P), slice(0, P), stop=t == TILES - 1)
                    last = add(0, slice(P, 2 * P), slice(P * t, P * t + P), stop=t == TILES - 1)
                    yield
                    if t > 1:
                        last = add(1, slice(256, 320), slice(P * t - 64, P * t), stop=t == TILES - 1)
                    if t < TILES - 1:
                        last = add(2, slice(256, 320), slice(P * t + P, P * t + 192))
                last.then_inc(pv_done[q % 3], 1)

            def turn_out(uses, b, hf, g):
                G = 4 * b + 2 * hf + g
                pe.wait_ge(ot_full, G + 1)
                for j in range(2):
                    pe.wait_ge(work_used[0], uses.next(0))
                    for t in range(HALF):
                        last = nc.tensor.transpose(WORK[0][:, P * t:P * t + P], oT[:, j, P * t:P * t + P], ident[:])
                    last.then_inc(work_full[0], 1)

            def first():
                uses = Uses([0, 0])
                for i in range(MAX_SLOTS):
                    if i in (0, MAX_SLOTS // 2):
                        pe.wait_ge(stack_in[0][i > 0], 96)
                    max_slot(uses, i, 0)
                shift(uses, 0, 0)

            def unit(b, hf, ahead, prior):
                R = 2 * b + hf
                uses = Uses([R0_BEFORE + R0_ROUND * R, R1_MAX + R1_ROUND * R])
                if not prior:
                    uses.n[0] = 2
                pe.wait_ge(m_in[hf], 32 * (b + 1))
                for q in range(UNIT_STEPS + (0 if ahead else 1)):
                    slots = iter(range(MAX_PER_STEP * q, min(MAX_PER_STEP * (q + 1), MAX_SLOTS)) if ahead else ())

                    def more(n=1):
                        for _, i in zip(range(n), slots):
                            if i in (0, MAX_SLOTS // 2):
                                pe.wait_ge(stack_in[ahead[1]][i > 0], 96 * (ahead[0] + 1))
                            max_slot(uses, i, ahead[1])

                    if q < UNIT_STEPS:
                        scores(b, hf, q, 0)
                    more()
                    if q < UNIT_STEPS:
                        scores(b, hf, q, 1)
                    more()
                    ending = (b, hf, q - 1) if q else (*prior, UNIT_STEPS - 1) if prior else None
                    if ending:
                        for _ in values(*ending):
                            more()
                    more(MAX_PER_STEP)
                    if q == PRIOR_OUT_AT and prior:
                        turn_out(uses, *prior, 1)
                    if q == OUT_AT:
                        turn_out(uses, b, hf, 0)
                    if q == SHIFT_AT and ahead:
                        shift(uses, *ahead)
                if not ahead:
                    turn_out(uses, b, hf, 1)

            rounds(pe, first, unit)

            for j in range(2):
                pe.wait_ge(att_free[j], 4 * BATCH)

            pe.wait_ge(late_consts, 1)
            pe.wait_ge(xw_in, 128)
            for m in range(CHUNKS):
                for c in range(CHUNKS):
                    last = nc.tensor.matmul(ps[:, m, 0:BATCH * KEYS], xw[1][:, c, P * m:P * m + P], ctx_sb[:, c, :], start=(c == 0), stop=(c == 1))
                last.then_inc(kc_made, 1)
            for b in range(BATCH):
                for c in range(CHUNKS):
                    last = nc.tensor.matmul(ps[0:KEYS, 4 + b // 2, 256 * (b % 2):256 * (b % 2) + 256], ctx_sb[:, c, KEYS * b:KEYS * b + KEYS],
                                            xw[2][:, c, :], start=(c == 0), stop=(c == 1))
            last.then_inc(gv_made, 1)
            pe.wait_ge(kc_kept, 2)
            for m in range(CHUNKS):
                for c in range(CHUNKS):
                    last = nc.tensor.matmul(ps[:, 2 + m, 0:BATCH * KEYS], xw[0][:, c, P * m:P * m + P], KcT[:, c, :], start=(c == 0), stop=(c == 1))
            last.then_inc(gv_made, 1)
            for c in range(CHUNKS):
                last = nc.tensor.matmul(ps[0:1, 6, 0:BATCH * KEYS], xb_sb[:, c:c + 1], KcT[:, c, :], start=(c == 0), stop=(c == 1))
            last.then_inc(gv_made, 1)
            pe.wait_ge(gv_kept, 2)

            def turn(n, src, base, ready, copied, turned):
                pe.wait_ge(ready, n + 1)
                need(pe, copied, n)
                for c in range(CHUNKS):
                    for t in range(HALF):
                        last = nc.tensor.transpose(ps[:, base + c, P * t:P * t + P], src[:, t, P * c:P * c + P], ident[:])
                last.then_inc(turned, 1)

            def gates(n):
                pe.wait_ge(xT3_copied, n + 1)
                for t in range(HALF):
                    for c in range(CHUNKS):
                        last = nc.tensor.matmul(ps[:, 0, 320 + EXPERTS * t:320 + EXPERTS * t + EXPERTS], xT3[:, c, P * t:P * t + P], gate_sb[:, c, :],
                                                start=(c == 0), stop=(c == 1))
                last.then_inc(lg_made, 1)

            turn(0, xn2, 1, xn2_ready, xT2_copied, turned2)

            def step(b, s, inner=False):
                n = halves_at(b, s)
                first, last_ = not inner and s == 0, not inner and s == 1
                pe.wait_ge(xT2_copied, n + 1)
                if not first:
                    pe.wait_ge(lg_kept, n - 1) if not isinstance(n, int) else need(pe, lg_kept, n - 1)
                for t in range(HALF):
                    S = ps[:, 0, KEYS * t:KEYS * t + KEYS]
                    for c in range(CHUNKS):
                        nc.tensor.matmul(S, xT2[s][:, c, P * t:P * t + P], G[:, c, bass.ds(KEYS * b, KEYS)], start=(c == 0), stop=False)
                    last = nc.tensor.matmul(S, ones[:], g0[:, bass.ds(KEYS * b, KEYS)], start=False, stop=True)
                last.then_inc(cs_made, 1)
                if not last_:
                    turn(n + 1, xn2, 1, xn2_ready, xT2_copied, turned2)
                pe.wait_ge(cp_ready, n + 1)
                for t in range(HALF):
                    last = nc.tensor.transpose(ps[0:KEYS, 3, P * t:P * t + P], cp[:, t, :], ident[:])
                last.then_inc(cp_turned, 1)
                if not first:
                    turn(n - 1, xn3[1 - s], 6, xn3_ready, xT3_copied, turned3)
                pe.wait_ge(cpT_copied, n + 1)
                for t in range(HALF):
                    last = nc.tensor.matmul(ps[:, 4 + t // 2, 256 * (t % 2):256 * (t % 2) + 256], cpT[:, P * t:P * t + P], Vc[:, b, :], start=True, stop=True)
                last.then_inc(cv_made, 1)
                if not first:
                    gates(n - 1)

            each_half(pe, step)
            pe.wait_ge(lg_kept, 2 * BATCH - 1)
            turn(2 * BATCH - 1, xn3[1], 6, xn3_ready, xT3_copied, turned3)
            gates(2 * BATCH - 1)
            pe.wait_ge(gates_ready, 1)
            nc.tensor.matmul(ps[:, 1, 0:ALL_TILES * EXPERTS], before[:], chosen16[:].rearrange("p t e -> p (t e)"), start=True, stop=True)
            nc.tensor.matmul(ps[:, 2, 0:ALL_TILES * EXPERTS], every[:], chosen16[:].rearrange("p t e -> p (t e)"), start=True, stop=True).then_inc(ranked, 1)
            pe.wait_ge(low_made, EXPERTS + 1)
            pe.wait_ge(ids_ready, 2)

            PARTS = ((w_hi, 0), (w_lo, 0), (w_hi, 1))

            def turn_x(t, first):
                n = first + t.n
                pe.wait_ge(rows_in[t.k], 16 * (first // BUFS + t.quad + 1))
                need(pe, x_lo_made, n - 1)
                for c in range(CHUNKS):
                    for j in range(2):
                        last = nc.tensor.transpose(ps[:, t.k % 2, GROUP * c + P * j:GROUP * c + P * j + P], blk_rows[t.k][:, j, P * c:P * c + P], ident[:])
                last.then_inc(x_turned, 1)

            def ff_step(shared, first):
                def expert(of):
                    return EXPERTS if shared else pe.value_load(blk_e[0:1, bass.ds(of.n, 1)], min_val=0, max_val=EXPERTS - 1)

                def step(i, known):
                    if exists(i + 1, known):
                        turn_x(i + 1, first)
                    if exists(i, known):
                        n, r = first + i.n, i.k % 2
                        e = expert(i)
                        pe.wait_ge(x_hi_made, n + 1)
                        pe.wait_ge(x_lo_made, n + 1)
                        need(pe, h_made, n - 1)
                        for which, base, done in ((0, 2, a_made), (1, 4, b_made)):
                            for m in range(CHUNKS):
                                for c in range(CHUNKS):
                                    for j, (w, lo) in enumerate(PARTS):
                                        last = nc.tensor.matmul(ps[:, base + r, GROUP * m:GROUP * m + GROUP], w[:, e, which, c, P * m:P * m + P],
                                                                (x_lo if lo else x_hi)[r][:, c, :], start=(c == 0 and j == 0), stop=(c == 1 and j == 2))
                            last.then_inc(done, 1)
                    a = i + -1
                    if exists(a, known):
                        n, r = first + a.n, a.k % 2
                        e = expert(a)
                        pe.wait_ge(h_hi_made, n + 1)
                        pe.wait_ge(h_lo_made, n + 1)
                        need(pe, y_read, n - 1)
                        for t in range(2):
                            for c in range(CHUNKS):
                                for j, (w, lo) in enumerate(PARTS):
                                    last = nc.tensor.matmul(ps[:, 6 + r, DIM * t:DIM * t + DIM], (h_lo if lo else h_hi)[r][:, c, P * t:P * t + P],
                                                            w[:, e, 2, c, :], start=(c == 0 and j == 0), stop=(c == 1 and j == 2))
                        last.then_inc(y_made, 1)
                return step

            turn_x(Block(0, 0), 0)
            each_block(pe, ff_step(True, 0), SHARED_BLOCKS)
            turn_x(Block(0, 0), SHARED_BLOCKS)
            each_block(pe, ff_step(False, SHARED_BLOCKS), BLOCKS)



def kernel(**inputs):
    import numpy as _np
    import concourse.bacc as _bacc
    from concourse import mybir as _mybir
    from concourse.bass_utils import run_bass_kernel_spmd as _run

    nc = _bacc.Bacc("TRN2", target_bir_lowering=False, num_devices=1)
    f = lambda n: inputs["L0_ffn_" + n]
    up, gate, down = (_np.concatenate([f(n), f("s" + n)[None]]) for n in ("w1", "w3", "w2"))
    cols = lambda n: _np.concatenate([f(n), f("s" + n)[None]]).reshape(EXPERTS + 1, CHUNKS, P).transpose(2, 0, 1).reshape(P, -1)
    laid = dict(x=inputs["x"].reshape(BATCH * TOKENS, DIM),
                wq=inputs["L0_attn_Wq"].T, wk=inputs["L0_attn_Wk"].T, wv=inputs["L0_attn_Wv"].T,
                bq=inputs["L0_attn_bq"], bk=inputs["L0_attn_bk"], bv=inputs["L0_attn_bv"],
                ctxT=inputs["ctx_1024"].reshape(BATCH * KEYS, DIM).T,
                xwqT=inputs["L0_xattn_Wq"].T, xwk=inputs["L0_xattn_Wk"], xwv=inputs["L0_xattn_Wv"],
                xbq=inputs["L0_xattn_bq"], xbk=inputs["L0_xattn_bk"], xbv=inputs["L0_xattn_bv"],
                gateT=f("gate_w").T, w_all=_np.stack([up, gate, down], 1).reshape(EXPERTS + 1, 3 * DIM, DIM),
                b1=cols("b1"), b3=cols("b3"), b2=_np.concatenate([f("b2"), f("sb2")[None]]))
    arrays = {k: _np.ascontiguousarray(v) for k, v in laid.items()}
    args = [nc.dram_tensor("in_" + k, a.shape, _mybir.dt.from_np(a.dtype), kind="ExternalInput").ap() for k, a in arrays.items()]
    out = nc.dram_tensor("y", (BATCH * TOKENS, DIM), _mybir.dt.float32, kind="ExternalOutput").ap()
    program(nc, *args, out)
    r = _run(nc, [{"in_" + k: a for k, a in arrays.items()}], core_ids=[0])
    return _np.asarray(r.results[0]["y"]).reshape(BATCH, TOKENS, DIM)
```

```python
import numpy as np
import concourse.bass as bass
from concourse import mybir
from contextlib import ExitStack

BATCH, TOKENS, DIM = 4, 1024, 256
HEADS, HEAD_DIM, BLOCK = 16, 16, 64
KEYS = 77
P = 128
TILES = TOKENS // P
HALF = 4
CHUNKS = DIM // P
HH = HEADS // 2
VW = HEAD_DIM + 1
VPAD = HH * VW + 32 - VW
STEPS = TILES + 1
UNIT_STEPS = 2 * STEPS
EPS = 1e-5
SCALE = HEAD_DIM ** -0.5
SHIFT = 64.0
MAX_SLOTS = HH * STEPS
R0_MAX, R1_MAX = MAX_SLOTS // 2, MAX_SLOTS // 2
R0_FIRST, R0_ROUND = R0_MAX + 1, R0_MAX + 5
R0_BEFORE = R0_FIRST - 2
R1_ROUND = R1_MAX
SHIFT_ROW = P - 2
OUT_AT = UNIT_STEPS - 2
PRIOR_OUT_AT = 2
SHIFT_AT = UNIT_STEPS - 3
PER_STEP = [4 if q - PRIOR_OUT_AT in (0, 1) else 5 for q in range(SHIFT_AT)]
TAKEN_BY = [min(sum(PER_STEP[:q]), MAX_SLOTS) for q in range(UNIT_STEPS + 2)]
assert TAKEN_BY[SHIFT_AT] == MAX_SLOTS

ALL_TILES = BATCH * TILES
EXPERTS, TOP_K = 8, 2
GROUP = 2 * P
SHARED_BLOCKS = BATCH * TOKENS // GROUP
BLOCKS = -(-(BATCH * TOKENS * TOP_K // GROUP + EXPERTS - 1) // 4) * 4
LIST_BLOCKS = BATCH * TOKENS // GROUP
ID_COL, GATE_COL = DIM, DIM + 1
ROW = GATE_COL + EXPERTS
NO_TOKEN = 1 << 20
W_SCALE = 16.0
BUFS = 8


def work0_uses(ahead, what, j=0):
    def maxima(step):
        return -(-TAKEN_BY[step + 1] // 2) if ahead else 0
    shift = int(bool(ahead))
    return {"prior_out1": maxima(PRIOR_OUT_AT + j) + j + 1, "shift": R0_MAX + 3, "out0": maxima(OUT_AT + j) + shift + j + 3, "out1": j + 5}[what]


def need(engine, sem, value):
    if not isinstance(value, int) or value > 0:
        engine.wait_ge(sem, value)


def program(nc, x, wq, wk, wv, bq, bk, bv, ctxT, xwqT, xwk, xwv, xbq, xbk, xbv, gateT, w_all, b1, b3, b2, out):
    f32, f16, i32, u32 = mybir.dt.float32, mybir.dt.float16, mybir.dt.int32, mybir.dt.uint32
    ALU, ACT, AX = mybir.AluOpType, mybir.ActivationFunctionType, mybir.AxisListType
    qk_dram = nc.dram_tensor("qk_parts", [BATCH, 2, 4, P, TOKENS], f16, kind="Internal").ap()
    v_dram = nc.dram_tensor("v_rows", [BATCH, 2, TILES, P, HH * VW], f32, kind="Internal").ap()
    slots = nc.dram_tensor("slots", [BLOCKS * GROUP, ROW], f32, kind="Internal").ap()
    with ExitStack() as ctx:
        def sb(name, shape, dt=f32):
            return ctx.enter_context(nc.sbuf_tensor(name, shape, dt))

        def sem(name):
            return ctx.enter_context(nc.semaphore(name))

        def sems(name, n):
            return [sem(f"{name}{i}") for i in range(n)]

        X = sb("x_rows", [P, BATCH * TILES, DIM])
        ident = sb("ident", [P, P])
        stats, stats3 = sb("stats", [P, HALF, 6]), sb("stats3", [P, HALF, 6])
        var_eps, var_eps3, halves_neg = (sb(name, [P, HALF]) for name in ("var_eps", "var_eps3", "halves_neg"))
        ps = ctx.enter_context(nc.psum_tensor("banks", [P, 8, 512], f32))
        ST = [ps[:, 0:2, :], ps[:, 2:4, :]]
        PO = ps[:, 4:6, :]
        WORK = [ps[:, 6, :], ps[:, 7, :]]

        mv2, rs2 = sb("mv2", [P, HALF, 2]), sb("rs2", [P, HALF])
        G = sb("G", [P, CHUNKS, BATCH * KEYS])
        g0 = sb("g0", [1, BATCH * KEYS])
        ones = sb("ones", [1, P])
        Vc = sb("Vc", [P, BATCH, DIM])
        gate_sb = sb("gate_sb", [P, CHUNKS, EXPERTS])

        with ExitStack() as early:
            def sb(name, shape, dt=f32):
                return early.enter_context(nc.sbuf_tensor(name, shape, dt))

            w_sb = [sb(f"w{n}_sb", [P, CHUNKS, DIM]) for n in "qkv"]
            qk_bias = sb("qk_bias", [P, 4])
            bv_all = sb("bv_all", [P, DIM])
            ident16 = sb("ident16", [P, P], f16)
            meanvar = [sb(f"meanvar{i}", [P, HALF, 2]) for i in range(2)]
            rstd = [sb(f"rstd{i}", [P, HALF]) for i in range(2)]
            qk_hi = [sb(f"qk_hi{i}", [P, 4, HALF * P], f16) for i in range(2)]
            qk_lo = [sb(f"qk_lo{i}", [P, 4, HALF * P], f16) for i in range(2)]
            v_out = [sb(f"v_out{i}", [P, HALF, HEADS, VW]) for i in range(2)]
            Kst = [sb(f"k_stack{i}", [P, HH, TOKENS], f16) for i in range(2)]
            Qst = [sb(f"q_stack{i}", [P, HH, TOKENS], f16) for i in range(2)]
            V = [sb(f"v{i}", [P, 3, TILES, VPAD]) for i in range(2)]
            probs = [sb(f"probs{i}", [P, 4, 512]) for i in range(3)]
            xn = [probs[0][:, 2 * i:2 * i + 2, :].rearrange("p a (t d) -> p (a t) d", d=DIM) for i in range(2)]
            xnT = [probs[1][:, 2 * i:2 * i + 2, :] for i in range(2)]
            fills = probs[2][:, 0:2, :].bitcast(f16)
            oT = sb("oT", [P, 2, 512])
            ctx_sb = sb("ctx_sb", [P, CHUNKS, BATCH * KEYS])
            xb_sb = sb("xb_sb", [P, 2 * CHUNKS])
            xbv_all = oT[0:KEYS, 0, 0:DIM]
            KcT = sb("KcT", [P, CHUNKS, BATCH * KEYS])
            xw = [sb(f"xw{i}", [P, CHUNKS, DIM]) for i in range(3)]
            mx = sb("mx", [P, HH, STEPS])
            mm = sb("mm", [P, P], f16)
            mT = [sb(f"mT{i}", [P, P], f16) for i in range(2)]
            rcp = sb("rcp", [P, HALF, 4])
            att = [sb(f"att{i}", [P, HALF, 4, HEAD_DIM]) for i in range(2)]


        def sb(name, shape, dt=f32):
            return ctx.enter_context(nc.sbuf_tensor(name, shape, dt))

        rows = sb("rows", [P, ALL_TILES, ROW])
        mv3, rs3 = sb("mv3", [P, HALF, 2]), sb("rs3", [P, HALF])
        xn2 = sb("xn2", [P, HALF, DIM])
        xn3 = [sb(f"xn3{i}", [P, HALF, DIM]) for i in range(2)]
        xT2 = [sb(f"xT2{i}", [P, CHUNKS, HALF * P]) for i in range(2)]
        xT3 = sb("xT3", [P, CHUNKS, HALF * P])
        neg_max, row_sum, row_rec = sb("neg_max", [P, HALF]), sb("row_sum", [P, HALF]), sb("row_rec", [P, HALF])
        cp = sb("cp", [P, HALF, P])
        cpT = sb("cpT", [P, HALF * P])
        logits = sb("logits", [P, ALL_TILES, EXPERTS])
        w_hi = sb("w_hi", [P, EXPERTS + 1, 3, CHUNKS, DIM], f16)
        w_lo = sb("w_lo", [P, EXPERTS + 1, 3, CHUNKS, DIM], f16)
        w_raw = [sb(f"w_raw{i}", [P, 3, CHUNKS, DIM]) for i in range(2)]
        b1_sb, b3_sb = sb("b1_sb", [P, EXPERTS + 1, CHUNKS]), sb("b3_sb", [P, EXPERTS + 1, CHUNKS])
        b2_all = sb("b2_all", [P, EXPERTS + 1, DIM])
        token_id = sb("token_id", [P, ALL_TILES], i32)
        blank = sb("blank", [P, ROW])
        e_i, e_f = sb("e_i", [P, EXPERTS], i32), sb("e_f", [P, EXPERTS])
        s_i, s_f = sb("s_i", [P, LIST_BLOCKS], i32), sb("s_f", [P, LIST_BLOCKS])
        blk_i, blk_f = sb("blk_i", [1, BLOCKS], i32), sb("blk_f", [1, BLOCKS])
        before = sb("before", [P, P], f16)
        every = sb("every", [P, P], f16)
        T8 = [P, ALL_TILES, EXPERTS]
        gate_probs, oh, chosen16 = sb("gate_probs", T8), [sb(f"one_hot{i}", T8) for i in range(2)], sb("chosen16", T8, f16)
        t8a, t8b = sb("t8a", T8), sb("t8b", T8)
        t1 = sb("t1", [P, ALL_TILES])
        cnt = [sb(f"cnt{i}", T8) for i in range(2)]
        nb_cmp = sb("nb_cmp", [P, EXPERTS, LIST_BLOCKS])
        nb = [sb(f"nb{i}", [P, EXPERTS]) for i in range(3)]
        list_at = sb("list_at", [P, EXPERTS])
        slot_f, slot = sb("slot_f", [P, TOP_K, ALL_TILES]), sb("slot", [P, TOP_K, ALL_TILES], u32)
        blk_cmp = sb("blk_cmp", [1, BLOCKS, EXPERTS - 1])
        blk_e = sb("blk_e", [1, BLOCKS], i32)
        blk_rows = [sb(f"blk_rows{i}", [P, 2, ROW]) for i in range(BUFS // 2)]
        blk_rows += [w_raw[i // 2][:].rearrange("p a c d -> p (a c d)")[:, 2 * ROW * (i % 2):2 * ROW * (i % 2 + 1)].rearrange("p (t c) -> p t c", t=2)
                     for i in range(BUFS // 2)]
        x_hi, x_lo, h_hi, h_lo = ([xT2[i // 2][:, i % 2, :].bitcast(f16)[:, 512 * j:512 * j + 512].rearrange("p (c t) -> p c t", c=CHUNKS)
                                   for j in range(2)] for i in range(4))
        sil, h_f = ([xn3[i][:, 2 * j:2 * j + 2, :] for j in range(2)] for i in range(2))
        y_sb = [xn2[:, 2 * j:2 * j + 2, :] for j in range(2)]

        eps_added = sem("eps_added")
        fills_ready, filled_in = sem("fills_ready"), sem("filled_in")
        waited_apart = sem("waited_apart")
        consts = sem("consts")
        w_in, x_in = sem("w_in"), sem("x_in")
        ln_step, var_ready, rstd_ready, xn_ready, turned, xT_copied = sem("ln_step"), sem("var_ready"), sem("rstd_ready"), sem("xn_ready"), sems("turned", 2), sem("xT_copied")
        qk_made, hi_made, qk_split = sem("qk_made"), sem("hi_made"), sem("qk_split")
        v_made, v_kept = sems("v_made", 2), sem("v_kept")
        qk_stored, v_stored = sems("qk_stored", 2), sems("v_stored", 2)
        stack_in, v_in, m_in = [sems(f"stack_in{i}_", 2) for i in range(2)], sems("v_in", 2), sems("m_in", 2)
        st_full, exped, pv_done = sems("st_full", 2), sems("exped", 2), sems("pv_done", 3)
        ot_full, rcp_made = sem("ot_full"), sem("rcp_made")
        work_full, work_used = sems("work_full", 2), sems("work_used", 2)
        dve_step, att_free = sem("dve_step"), sems("att_free", 2)
        late_consts, xw_in = sem("late_consts"), sem("xw_in")
        kc_made, kc_kept, gv_made, gv_kept = sem("kc_made"), sem("kc_kept"), sem("gv_made"), sem("gv_kept")
        stat2, var2, rstd2, xn2_ready, turned2, xT2_copied = (sem(n) for n in ("stat2", "var2", "rstd2", "xn2_ready", "turned2", "xT2_copied"))
        stat3, var3, rstd3, xn3_ready, turned3, xT3_copied = (sem(n) for n in ("stat3", "var3", "rstd3", "xn3_ready", "turned3", "xT3_copied"))
        late_eps, rows_kept = sem("late_eps"), sems("rows_kept", 2)
        cs_made, neg_ready, cp_ready, cp_turned, cpT_copied, cv_made, rec_ready, x2_ready = (
            sem(n) for n in ("cs_made", "neg_ready", "cp_ready", "cp_turned", "cpT_copied", "cv_made", "rec_ready", "x2_ready"))
        pads = sem("pads")
        lg_made, lg_kept = sem("lg_made"), sem("lg_kept")
        raw_in, scaled, low_made = sems("raw_in", 2), sem("scaled"), sem("low_made")
        ff_bias_in, slots_blank = sem("ff_bias_in"), sem("slots_blank")
        route, exp_done, ranked, ids_ready, gates_ready = (sem(n) for n in ("route", "exp_done", "ranked", "ids_ready", "gates_ready"))
        dispatched = sem("dispatched")
        rows_in, scattered = sems("blk_rows_in", BUFS), sems("scattered", BUFS)
        x_turned, x_hi_made, x_lo_made = sem("x_turned"), sem("x_hi_made"), sem("x_lo_made")
        a_made, b_made, sil_made, h_made, h_hi_made, h_lo_made = (sem(n) for n in ("a_made", "b_made", "sil_made", "h_made", "h_hi_made", "h_lo_made"))
        y_made, y_read, y_ready, shared_bias_in_x = sem("y_made"), sem("y_read"), sem("y_ready"), sem("shared_bias_in_x")
        base_out = sem("base_out")
        block = ctx.enter_context(nc.Block())

        def x_parts(ap, b, sb_rows):
            base = b * TOKENS
            yield sb_rows[0:64, 0, :], ap[bass.ds(base, 64), :]
            yield sb_rows[64:128, 0, :], ap[bass.ds(base + TOKENS - 64, 64), :]
            yield sb_rows[:, 1:TILES, :], ap[bass.ds(base + 64, TOKENS - P), :].rearrange("(t p) d -> p t d", p=P)

        def halves(eng, before, after):
            before(0, 0)
            with eng.Fori(0, BATCH - 1) as b:
                before(b, 1)
                after(b, 0)
                before(b + 1, 0)
                after(b, 1)
            before(BATCH - 1, 1)
            after(BATCH - 1, 0)
            after(BATCH - 1, 1)

        def rounds(eng, first, unit):
            first()
            unit(0, 0, (0, 1), None)
            with eng.Fori(0, BATCH - 1) as b:
                unit(b, 1, (b + 1, 0), (b, 0))
                unit(b + 1, 0, (b + 1, 1), (b, 1))
            unit(BATCH - 1, 1, None, (BATCH - 1, 0))

        def each_half(eng, step):
            step(0, 0)
            with eng.Fori(0, BATCH - 1) as b:
                step(b, 1, inner=True)
                step(b + 1, 0, inner=True)
            step(BATCH - 1, 1)

        def halves_at(b, s):
            return 2 * b + s

        def wait_apart(engine, sem, value):
            engine.wait_ge(sem, value)
            engine.sem_inc(waited_apart, 1)

        class Block:
            def __init__(self, quad, k):
                self.quad, self.k = quad, k
                self.n = BUFS * quad + k

            def __add__(self, d):
                up, k = divmod(self.k + d, BUFS)
                return Block(self.quad + up, k)

        def each_block(eng, step, count):
            for i in range(3):
                step(Block(0, i), range(count))
            with eng.Fori(0, (count - BUFS) // BUFS) as quad:
                for k in range(3, 3 + BUFS):
                    step(Block(quad, 0) + k, None)
            for i in range(3 + count - BUFS, count + 2):
                step(Block(i // BUFS, i % BUFS), range(count))

        def exists(block, known):
            return known is None or block.n in known

        class Uses:
            def __init__(self, base, ahead_of=0):
                self.base, self.n, self.ahead_of = base, [0, 0], ahead_of

            def next(self, bank):
                self.n[bank] += 1
                return self.base[bank] + self.n[bank] - self.ahead_of

        @block.gpsimd
        def _(pool):
            nc.gpsimd.memset(ident[:], 0.0).then_inc(consts, 1)
            pool.wait_ge(consts, 1)
            nc.gpsimd.affine_select(out=ident[:], in_=ident[:], compare_op=ALU.not_equal, fill=1.0, base=0,
                                    pattern=[[-1, P]], channel_multiplier=1).then_inc(consts, 1)
            pool.wait_ge(consts, 2)
            nc.gpsimd.tensor_copy(ident16[:], ident[:]).then_inc(consts, 1)
            nc.gpsimd.memset(halves_neg[:], -0.5).then_inc(consts, 1)
            filled = 4

            def fill(ap, value):
                nonlocal filled
                pool.wait_ge(consts, filled)
                nc.gpsimd.memset(ap, value).then_inc(consts, 1)
                filled += 1

            for i in range(2):
                fill(v_out[i][:, :, :, HEAD_DIM:VW], 1.0)
            for i in range(2):
                fill(V[i][64:128, 1, :, :], 0.0)
                fill(V[i][0:64, 2, :, :], 0.0)
                fill(V[i][:, 0, :, HH * VW:VPAD], 0.0)
                fill(V[i][0:64, 1, :, HH * VW:VPAD], 0.0)
                fill(V[i][64:128, 2, :, HH * VW:VPAD], 0.0)

            fill(ones[:], 1.0)
            pool.wait_ge(consts, filled)

            def rsqrt(b, s):
                n = 2 * b + s
                wait_apart(pool, var_ready, n + 1)
                nc.gpsimd.tensor_scalar(var_eps[:], meanvar[s][:, :, 1], EPS, None, ALU.add).then_inc(eps_added, 1)
                pool.wait_ge(eps_added, n + 1)
                nc.gpsimd.tensor_tensor(rstd[s][:], var_eps[:], halves_neg[:], ALU.pow).then_inc(rstd_ready, 1)

            with pool.Fori(0, BATCH) as b:
                rsqrt(b, 0)
                rsqrt(b, 1)

            def shift_rows(b, hf, first=None):
                R = 2 * b + hf - 1
                wait_apart(pool, work_used[0], R0_BEFORE + R0_ROUND * R + work0_uses(True, "shift") if first is None else R0_FIRST)
                for part in range(2):
                    pool.dma_start(Qst[hf][SHIFT_ROW + part:SHIFT_ROW + part + 1, :, :].rearrange("o h (t q) -> o (h t) q", q=P),
                                   mT[hf][64 * part:64 * part + 64, :]).then_inc(m_in[hf], 16)

            def add_group(b, hf, g, at):
                for j in range(2):
                    pool.wait_ge(work_used[0], at[j])
                    rows = X[:, bass.ds(b * TILES + HALF * j, HALF), (hf * HH + 4 * g) * HEAD_DIM:(hf * HH + 4 * g + 4) * HEAD_DIM]
                    nc.gpsimd.tensor_tensor(rows, rows, att[j][:].rearrange("p t h d -> p t (h d)"), ALU.add).then_inc(att_free[j], 1)

            def unit(b, hf, ahead, prior):
                before = R0_BEFORE + R0_ROUND * (2 * b + hf)
                if prior:
                    add_group(*prior, 1, [before + work0_uses(ahead, "prior_out1", j) for j in range(2)])
                if ahead:
                    shift_rows(*ahead)
                add_group(b, hf, 0, [before + work0_uses(ahead, "out0", j) for j in range(2)])
                if not ahead:
                    add_group(b, hf, 1, [before + work0_uses(ahead, "out1", j) for j in range(2)])

            rounds(pool, lambda: shift_rows(0, 0, first=True), unit)

            def norm_scale(n, turn, var, mv, var_eps, rs, ready):
                wait_apart(pool, var, n + 1)
                nc.gpsimd.tensor_scalar(var_eps[:], mv[:, :, 1], EPS, None, ALU.add).then_inc(late_eps, 1)
                pool.wait_ge(late_eps, turn + 1)
                nc.gpsimd.tensor_tensor(rs[:], var_eps[:], halves_neg[:], ALU.pow).then_inc(ready, 1)

            norm_scale(0, 0, var2, mv2, var_eps, rs2, rstd2)
            for j in range(2):
                pool.wait_ge(att_free[j], 4 * BATCH)

            done = 0

            def made(instruction):
                nonlocal done
                instruction.then_inc(late_consts, 1)
                done += 1
                pool.wait_ge(late_consts, done)

            made(nc.gpsimd.memset(every[:], 1.0))
            made(nc.gpsimd.affine_select(out=before[:], in_=every[:], compare_op=ALU.is_gt, fill=0.0, base=0,
                                         pattern=[[1, P]], channel_multiplier=-1))
            made(nc.gpsimd.iota(e_i[:], pattern=[[1, EXPERTS]], base=-EXPERTS, channel_multiplier=0))
            made(nc.gpsimd.tensor_copy(e_f[:], e_i[:]))
            made(nc.gpsimd.iota(s_i[:], pattern=[[GROUP, LIST_BLOCKS]], base=0, channel_multiplier=0))
            made(nc.gpsimd.tensor_copy(s_f[:], s_i[:]))
            made(nc.gpsimd.iota(blk_i[:], pattern=[[1, BLOCKS]], base=0, channel_multiplier=0))
            made(nc.gpsimd.tensor_copy(blk_f[:], blk_i[:]))
            made(nc.gpsimd.iota(token_id[:].rearrange("p (b t) -> p b t", b=BATCH), pattern=[[TOKENS, BATCH], [P, TILES]],
                                base=-BLOCK, channel_multiplier=1))
            first_tiles = token_id[:].rearrange("p (b t) -> p b t", b=BATCH)[:, :, 0]
            made(nc.gpsimd.iota(first_tiles[0:BLOCK], pattern=[[TOKENS, BATCH]], base=0, channel_multiplier=1))
            made(nc.gpsimd.iota(first_tiles[BLOCK:P], pattern=[[TOKENS, BATCH]], base=TOKENS - BLOCK, channel_multiplier=1))
            made(nc.gpsimd.tensor_copy(rows[:, :, ID_COL:ID_COL + 1].bitcast(i32), token_id[:].unsqueeze(2)))
            made(nc.gpsimd.memset(blank[:], 0.0))
            made(nc.gpsimd.memset(blank[:, ID_COL:ID_COL + 1].bitcast(i32), NO_TOKEN))

            def low_part(n, s):
                pool.wait_ge(scaled, n + 1)
                nc.gpsimd.tensor_tensor(w_lo[:, n, :, :, :].rearrange("p a c d -> p (a c d)"), w_raw[s][:].rearrange("p a c d -> p (a c d)"),
                                        w_hi[:, n, :, :, :].rearrange("p a c d -> p (a c d)"), ALU.subtract).then_inc(low_made, 1)

            def add_shared_bias(n):
                pool.wait_ge(xn3_ready, n + 1)
                tiles = X[:, bass.ds(HALF * n, HALF), :]
                nc.gpsimd.tensor_tensor(tiles, tiles, b2_all[:, EXPERTS:EXPERTS + 1, :].broadcast_to([P, HALF, DIM]), ALU.add).then_inc(shared_bias_in_x, 1)

            pool.wait_ge(ff_bias_in, 48)

            def step(b, s, inner=False):
                n = halves_at(b, s)
                last = not inner and s == 1
                if not last:
                    norm_scale(n + 1, 2 * n + 1, var2, mv2, var_eps, rs2, rstd2)
                if inner or last:
                    low_part(n - 1, 1 - s)
                norm_scale(n, 2 * n + 2 if not last else 2 * n + 1, var3, mv3, var_eps3, rs3, rstd3)
                if inner or last:
                    add_shared_bias(n - 1)

            each_half(pool, step)
            add_shared_bias(2 * BATCH - 1)
            low_part(EXPERTS - 1, 1)
            low_part(EXPERTS, 0)

            pool.wait_ge(ids_ready, 1)
            pool.wait_ge(gates_ready, 1)
            for s in range(2):
                pool.wait_ge(rows_kept[s], 16 * BATCH)
            pool.wait_ge(slots_blank, 16 * (BLOCKS // 4))
            for t in range(ALL_TILES):
                for k in range(TOP_K):
                    pool.indirect_dma_start(out=slots, out_offset=bass.IndirectOffsetOnAxis(ap=slot[:, k, t:t + 1], axis=0),
                                            in_=rows[:, t, :], in_offset=None, bounds_check=BLOCKS * GROUP - 1,
                                            oob_is_err=True).then_inc(dispatched, 16)

            pool.wait_ge(base_out, 48 * BATCH)

            def expert_step(i, known):
                if exists(i + -2, known):
                    y = i + -2
                    wait_apart(pool, y_ready, y.n + 1)
                    prior = y + -1
                    if not isinstance(y.n, int) or y.n > 0:
                        wait_apart(pool, scattered[prior.k], 32 * (prior.quad + 1))
                    for t in range(2):
                        pool.indirect_dma_start(out=out, out_offset=bass.IndirectOffsetOnAxis(
                            ap=blk_rows[y.k][:, t, ID_COL:ID_COL + 1].bitcast(u32), axis=0),
                            in_=y_sb[y.k % 2][:, t, :], in_offset=None, bounds_check=BATCH * TOKENS - 1, oob_is_err=False,
                            compute_op=ALU.add).then_inc(scattered[y.k], 16)

            each_block(pool, expert_step, BLOCKS)
            for k in range(BUFS):
                pool.wait_ge(scattered[k], 32 * (BLOCKS // BUFS))

        @block.sync
        def _(sp):
            for w, dram in zip(w_sb, (wq, wk, wv)):
                sp.dma_start(w[:], dram.rearrange("(c p) n -> p c n", p=P)).then_inc(w_in, 16)
            for i, bias in enumerate((bq, bk)):
                sp.dma_start(qk_bias[:, 2 * i:2 * i + 2], bias.rearrange("(c p) -> p c", p=P), allow_slow_non_contiguous=True).then_inc(w_in, 16)
            sp.dma_start(bv_all[:], bv.partition_broadcast(P)).then_inc(w_in, 16)
            for b in range(BATCH):
                for dst, src in x_parts(x, b, X[:, b * TILES:(b + 1) * TILES, :]):
                    sp.dma_start(dst, src).then_inc(x_in, 16)
                sp.wait_ge(x_in, 48 * (b + 1))
            def store(b, s):
                n = 2 * b + s
                cols = slice(s * 512, s * 512 + 512)
                sp.wait_ge(qk_split, 4 * n + 4)
                for part, src in enumerate((qk_hi[s], qk_lo[s])):
                    sp.dma_start(qk_dram[b, part, :, :, cols].rearrange("i p t -> p i t"),
                                 src[:]).then_inc(qk_stored[s], 16)
                sp.wait_ge(v_kept, 2 * n + 2)
                for hf in range(2):
                    sp.dma_start(v_dram[b, hf, s * HALF:(s + 1) * HALF, :, :].rearrange("t p c -> p t c"),
                                 v_out[s][:, :, hf * HH:(hf + 1) * HH, :].rearrange("p t h c -> p t (h c)")).then_inc(v_stored[s], 16)

            def load_unit(b, hf, again):
                for g in range(2):
                    if again:
                        sp.wait_ge(exped[1], UNIT_STEPS * (2 * b + hf - 2) + STEPS * (g + 1))
                    for dst, which, parts in ((Kst[hf], 1, (0, 0, 1)), (Qst[hf], 0, (1, 0, 0))):
                        for c, part in enumerate(parts):
                            sp.dma_start(dst[16 * c:16 * c + 16, 4 * g:4 * g + 4, :],
                                         qk_dram[b, part, 2 * which + hf, 64 * g:64 * g + 64, :].rearrange("(h d) t -> d h t", d=HEAD_DIM)).then_inc(stack_in[hf][g], 16)
                if again:
                    sp.wait_ge(pv_done[2], UNIT_STEPS // 3 * (2 * b + hf - 1))
                for c, rows in enumerate((slice(0, P), slice(0, 64), slice(64, P))):
                    sp.dma_start(V[hf][rows, c, :, 0:HH * VW], v_dram[b, hf, :, rows, :].rearrange("t p c -> p t c")).then_inc(v_in[hf], 16)

            for w, dram in zip((ctx_sb, *xw, gate_sb), (ctxT, xwqT, xwk, xwv, gateT)):
                sp.dma_start(w[:], dram.rearrange("(c p) n -> p c n", p=P)).then_inc(xw_in, 16)
            for i, bias in enumerate((xbq, xbk)):
                sp.dma_start(xb_sb[:, CHUNKS * i:CHUNKS * i + CHUNKS], bias.rearrange("(c p) -> p c", p=P), allow_slow_non_contiguous=True).then_inc(xw_in, 16)
            sp.dma_start(xbv_all, xbv.partition_broadcast(KEYS)).then_inc(xw_in, 16)
            sp.wait_ge(fills_ready, 2)
            for i in range(2):
                for st in (Kst[i], Qst[i]):
                    sp.dma_start(st[32:SHIFT_ROW, :, :], fills[32:SHIFT_ROW, 0:1, :].broadcast_to([SHIFT_ROW - 32, HH, TOKENS])).then_inc(filled_in, 16)
                sp.dma_start(Kst[i][SHIFT_ROW:P, :, :], fills[SHIFT_ROW:P, 1:2, :].broadcast_to([2, HH, TOKENS])).then_inc(filled_in, 16)

            with sp.Fori(0, 2) as b:
                store(b, 0)
                store(b, 1)
            for s in range(2):
                sp.wait_ge(qk_stored[s], 64)
                sp.wait_ge(v_stored[s], 64)
            sp.wait_ge(consts, 16)
            sp.wait_ge(filled_in, 96)
            load_unit(0, 0, False)
            load_unit(0, 1, False)
            with sp.Fori(2, BATCH) as b:
                store(b, 0)
                store(b, 1)
            for s in range(2):
                sp.wait_ge(qk_stored[s], 32 * BATCH)
                sp.wait_ge(v_stored[s], 32 * BATCH)
            with sp.Fori(1, BATCH) as b:
                load_unit(b, 0, True)
                load_unit(b, 1, True)

            for j in range(2):
                sp.wait_ge(att_free[j], 4 * BATCH)

            for bias, dram in ((b1_sb, b1), (b3_sb, b3)):
                sp.dma_start(bias[:].rearrange("p e c -> p (e c)"), dram).then_inc(ff_bias_in, 16)
            sp.dma_start(b2_all[:], b2.partition_broadcast(P)).then_inc(ff_bias_in, 16)

            def load_weights(e, s):
                sp.dma_start(w_raw[s][:].rearrange("p a c d -> p (a c) d"), w_all[e, :, :].rearrange("(a p) d -> p a d", p=P)).then_inc(raw_in[s], 16)

            load_weights(0, 0)
            load_weights(1, 1)
            sp.wait_ge(late_consts, 14)
            for i in range(BLOCKS // 4):
                rows_of = slots[8 * P * i:8 * P * i + 8 * P, :].rearrange("(t p) c -> p t c", p=P)
                sp.dma_start(rows_of, blank[:].unsqueeze(1).broadcast_to([P, 8, ROW])).then_inc(slots_blank, 16)

            def keep_rows(n, s):
                sp.wait_ge(xn3_ready, n + 1)
                sp.dma_start(rows[:, bass.ds(HALF * n, HALF), 0:DIM], xn3[s][:]).then_inc(rows_kept[s], 16)

            with sp.Fori(0, EXPERTS // 2 - 1) as half:
                for s in range(2):
                    keep_rows(2 * half + s, s)
                    sp.wait_ge(low_made, 2 * half + s + 1)
                    load_weights(2 * half + s + 2, s)
            keep_rows(EXPERTS - 2, 0)
            sp.wait_ge(low_made, EXPERTS - 1)
            load_weights(EXPERTS, 0)
            keep_rows(EXPERTS - 1, 1)

            def load_shared(at):
                sp.dma_start(blk_rows[at.k][:], rows[:, bass.ds(2 * at.n, 2), :]).then_inc(rows_in[at.k], 16)

            for s in range(2):
                sp.wait_ge(rows_kept[s], 16 * BATCH)
            sp.wait_ge(gates_ready, 1)
            for k in range(BUFS):
                if k == BUFS // 2:
                    sp.wait_ge(low_made, EXPERTS + 1)
                load_shared(Block(0, k))
            with sp.Fori(1, SHARED_BLOCKS // BUFS) as quad:
                for k in range(BUFS):
                    sp.wait_ge(x_turned, BUFS * quad + k - BUFS + 1)
                    load_shared(Block(quad, k))

            def load_expert(at):
                sp.dma_start(blk_rows[at.k][:], slots[bass.ds(GROUP * at.n, GROUP), :].rearrange("(t p) c -> p t c", p=P)).then_inc(rows_in[at.k], 16)

            sp.wait_ge(dispatched, 16 * TOP_K * ALL_TILES)
            for k in range(BUFS):
                sp.wait_ge(x_turned, SHARED_BLOCKS - BUFS + k + 1)
                load_expert(Block(0, k))
            sp.wait_ge(y_read, SHARED_BLOCKS)
            for b in range(BATCH):
                for src, dst in x_parts(out, b, X[:, b * TILES:(b + 1) * TILES, :]):
                    sp.dma_start(dst, src).then_inc(base_out, 16)
            with sp.Fori(1, BLOCKS // BUFS) as quad:
                for k in range(BUFS):
                    sp.wait_ge(scattered[k], 32 * quad)
                    load_expert(Block(quad, k))
            sp.wait_ge(base_out, 48 * BATCH)

        @block.vector
        def _(dve):
            def moments(b, s):
                n = 2 * b + s
                dve.wait_ge(x_in, 48 * (b + 1))
                for t in range(HALF):
                    last = nc.vector.bn_stats(stats[:, t, :], X[:, b * TILES + s * HALF + t, :])
                last.then_inc(ln_step, 1)
                wait_apart(dve, ln_step, n + 1)
                for t in range(HALF):
                    last = nc.vector.bn_aggr(meanvar[s][:, t, :], stats[:, t, :])
                last.then_inc(var_ready, 1)

            def norm(b, s):
                n = 2 * b + s
                dve.wait_ge(rstd_ready, n + 1)
                dve.wait_ge(var_ready, n + 1)
                need(dve, turned[s], b)
                for t in range(HALF):
                    last = nc.vector.tensor_scalar(xn[s][:, t, :], X[:, b * TILES + s * HALF + t, :], meanvar[s][:, t, 0:1],
                                                   rstd[s][:, t:t + 1], ALU.subtract, ALU.mult)
                last.then_inc(xn_ready, 1)

            nc.vector.memset(fills[:, 0, :], 0.0).then_inc(fills_ready, 1)
            nc.vector.memset(fills[:, 1, :], SHIFT).then_inc(fills_ready, 1)
            nc.vector.memset(Vc[:], 0.0).then_inc(pads, 1)
            dve.wait_ge(pads, 1)
            dve.wait_ge(consts, 6)
            dve.wait_ge(w_in, 96)

            def split(b, s, ahead=None):
                n = 2 * b + s
                for i in range(4):
                    if ahead and i == 1:
                        moments(*ahead)
                    if ahead and i == 3:
                        norm(*ahead)
                    dve.wait_ge(hi_made, 4 * n + i + 1)
                    if i == 0:
                        dve.wait_ge(qk_stored[s], 32 * b)
                    nc.vector.scalar_tensor_tensor(out=qk_lo[s][:, i, :], in0=ps[:, i, :], scalar=qk_bias[:, i:i + 1],
                                                   in1=qk_hi[s][:, i, :], op0=ALU.add, op1=ALU.subtract).then_inc(qk_split, 1)
                for j in range(2):
                    dve.wait_ge(v_made[s], 2 * b + j + 1)
                    if j == 0:
                        dve.wait_ge(v_stored[s], 32 * b)
                    for t in range(2):
                        last = nc.vector.tensor_tensor(
                            v_out[s][:, 2 * j + t, :, 0:HEAD_DIM],
                            ps[:, 4 + j, 256 * t:256 * t + 256].rearrange("p (h d) -> p h d", d=HEAD_DIM),
                            bv_all[:].rearrange("p (h d) -> p h d", d=HEAD_DIM), ALU.add)
                    last.then_inc(v_kept, 1)

            for s in range(2):
                moments(0, s)
                norm(0, s)
            with dve.Fori(0, BATCH - 1) as b:
                for s in range(2):
                    split(b, s, ahead=(b + 1, s))
            for s in range(2):
                split(BATCH - 1, s)

            def max_slot(uses, i):
                h, j = divmod(i, STEPS)
                r = i % 2
                dve.wait_ge(work_full[r], uses.next(r))
                width = 512 if j < 2 else 320
                col = (0, TILES)[j] if j < 2 else j - 1
                nc.vector.tensor_reduce(mx[:, h, col:col + 1], WORK[r][:, 0:width], AX.X, ALU.max).then_inc(work_used[r], 1)

            def shift(uses, b, hf):
                n = 2 * b + hf
                dve.wait_ge(work_used[0], uses.base[0] + uses.n[0])
                dve.wait_ge(work_used[1], uses.base[1] + uses.n[1])
                nc.vector.tensor_tensor(mx[:, :, 0:1], mx[:, :, 0:1], mx[:, :, TILES:TILES + 1], ALU.max).then_inc(dve_step, 1)
                dve.wait_ge(dve_step, 3 * n + 1)
                hi, lo = (mm[:, 64 * k:64 * k + 64].rearrange("p (h t) -> p h t", t=TILES) for k in range(2))
                nc.vector.tensor_scalar(hi, mx[:, :, 0:TILES], -1.0 / SHIFT, None, ALU.mult).then_inc(dve_step, 1)
                dve.wait_ge(dve_step, 3 * n + 2)
                nc.vector.scalar_tensor_tensor(out=lo, in0=mx[:, :, 0:TILES], scalar=-1.0 / SHIFT, in1=hi,
                                               op0=ALU.mult, op1=ALU.subtract).then_inc(dve_step, 1)
                dve.wait_ge(work_full[0], uses.next(0))
                dve.wait_ge(m_in[hf], 32 * b)
                nc.vector.tensor_copy(mT[hf][:], WORK[0].bitcast(f16)[:, 0:P]).then_inc(work_used[0], 1)

            def tiles_of(n):
                return [X[:, HALF * n + t, :] for t in range(HALF)]

            def tile_moments(n, stats, stat, var, mv):
                for t in range(HALF):
                    last = nc.vector.bn_stats(stats[:, t, :], tiles_of(n)[t])
                last.then_inc(stat, 1)
                wait_apart(dve, stat, n + 1)
                for t in range(HALF):
                    last = nc.vector.bn_aggr(mv[:, t, :], stats[:, t, :])
                last.then_inc(var, 1)

            def normalise(uses, b, hf, g, halves):
                G = 4 * b + 2 * hf + g
                for j in halves:
                    dve.wait_ge(work_full[0], uses.next(0))
                    o = WORK[0].rearrange("p (t h c) -> p t h c", t=HALF, h=4)
                    nc.vector.reciprocal(rcp[:], o[:, :, :, HEAD_DIM]).then_inc(rcp_made, 1)
                    dve.wait_ge(rcp_made, 2 * G + j + 1)
                    dve.wait_ge(att_free[j], G)
                    nc.vector.tensor_tensor(att[j][:], o[:, :, :, 0:HEAD_DIM],
                                            rcp[:].unsqueeze(3).broadcast_to([P, HALF, 4, HEAD_DIM]), ALU.mult).then_inc(work_used[0], 1)

            def first():
                uses = Uses([0, 0])
                for i in range(MAX_SLOTS):
                    max_slot(uses, i)
                shift(uses, 0, 0)
                dve.wait_ge(xw_in, 128)
                dve.wait_ge(gv_made, 3)
                for b in range(BATCH):
                    last = nc.vector.tensor_tensor(Vc[0:KEYS, b, :], ps[0:KEYS, 4 + b // 2, 256 * (b % 2):256 * (b % 2) + 256], xbv_all, ALU.add)
                last.then_inc(gv_kept, 1)

            def unit(b, hf, ahead, prior):
                R = 2 * b + hf
                uses = Uses([R0_BEFORE + R0_ROUND * R, R1_MAX + R1_ROUND * R])
                if not prior:
                    uses.n[0] = 2
                for q in range(UNIT_STEPS + 1):
                    if ahead:
                        for i in range(TAKEN_BY[q], TAKEN_BY[q + 1]):
                            max_slot(uses, i)
                    if q - PRIOR_OUT_AT in (0, 1) and prior:
                        normalise(uses, *prior, 1, [q - PRIOR_OUT_AT])
                    if q - OUT_AT in (0, 1):
                        normalise(uses, b, hf, 0, [q - OUT_AT])
                    if q == SHIFT_AT and ahead:
                        shift(uses, *ahead)
                if not ahead:
                    for j in range(2):
                        dve.wait_ge(att_free[j], 4)
                    tile_moments(0, stats, stat2, var2, mv2)
                    normalise(uses, b, hf, 1, range(2))

            rounds(dve, first, unit)

            for j in range(2):
                dve.wait_ge(att_free[j], 4 * BATCH)

            nc.vector.memset(cp[:, :, KEYS:P], 0.0).then_inc(pads, 1)
            def norm(n, mv, rs, rstd, dst, free, ready):
                tiles = tiles_of(n)
                dve.wait_ge(rstd, n + 1)
                for s, v in free:
                    dve.wait_ge(s, v)
                for t in range(HALF):
                    last = nc.vector.tensor_scalar(dst[:, t, :], tiles[t], mv[:, t, 0:1], rs[:, t:t + 1], ALU.subtract, ALU.mult)
                last.then_inc(ready, 1)

            norm(0, mv2, rs2, rstd2, xn2, [], xn2_ready)

            def step(b, s, inner=False):
                n = halves_at(b, s)
                last = not inner and s == 1
                dve.wait_ge(cs_made, n + 1)
                nc.vector.tensor_reduce(neg_max[:], ps[:, 0, 0:HALF * KEYS].rearrange("p (t k) -> p t k", k=KEYS), AX.X, ALU.max,
                                        negate=True).then_inc(neg_ready, 1)
                if not last:
                    tile_moments(n + 1, stats, stat2, var2, mv2)
                if inner or last:
                    norm3(n - 1, b - (1 - s), 1 - s)
                if not last:
                    norm(n + 1, mv2, rs2, rstd2, xn2, [(turned2, n + 1)], xn2_ready)
                dve.wait_ge(cp_ready, n + 1)
                nc.vector.reciprocal(row_rec[:], row_sum[:]).then_inc(rec_ready, 1)
                dve.wait_ge(rec_ready, n + 1)
                dve.wait_ge(cv_made, n + 1)
                for t in range(HALF):
                    tile_ = X[:, HALF * n + t, :]
                    lastx = nc.vector.scalar_tensor_tensor(out=tile_, in0=ps[:, 4 + t // 2, 256 * (t % 2):256 * (t % 2) + 256],
                                                           scalar=row_rec[:, t:t + 1], in1=tile_, op0=ALU.mult, op1=ALU.add)
                lastx.then_inc(x2_ready, 1)
                if inner or last:
                    keep_logits(n - 1)
                wait_apart(dve, x2_ready, n + 1)
                tile_moments(n, stats3, stat3, var3, mv3)

            def norm3(n, b, s):
                free = [] if isinstance(n, int) and n < 2 else [(rows_kept[s], 16 * b)]
                norm(n, mv3, rs3, rstd3, xn3[s], free, xn3_ready)

            def keep_logits(n):
                dve.wait_ge(lg_made, n + 1)
                nc.vector.tensor_copy(logits[:, bass.ds(HALF * n, HALF), :], ps[:, 0, 320:320 + HALF * EXPERTS].rearrange("p (t e) -> p t e", e=EXPERTS)).then_inc(lg_kept, 1)

            each_half(dve, step)
            norm3(2 * BATCH - 1, BATCH - 1, 1)
            keep_logits(2 * BATCH - 1)

            routed = 0

            def link(instruction):
                nonlocal routed
                instruction.then_inc(route, 1)
                routed += 1
                dve.wait_ge(route, routed)

            def per_expert(ap):
                return ap.unsqueeze(2).broadcast_to(T8)

            def per_tile(ap):
                return ap.unsqueeze(1).broadcast_to(T8)

            dve.wait_ge(late_consts, 14)
            dve.wait_ge(lg_kept, 2 * BATCH)
            link(nc.vector.tensor_reduce(t1[:], logits[:], AX.X, ALU.max))
            link(nc.vector.tensor_tensor(logits[:], logits[:], per_expert(t1[:]), ALU.subtract))
            dve.wait_ge(exp_done, 1)
            link(nc.vector.tensor_reduce(t1[:], gate_probs[:], AX.X, ALU.add))
            link(nc.vector.reciprocal(t1[:], t1[:]))
            link(nc.vector.tensor_tensor(gate_probs[:], gate_probs[:], per_expert(t1[:]), ALU.mult))
            left = gate_probs
            for k in range(TOP_K):
                link(nc.vector.tensor_reduce(t1[:], left[:], AX.X, ALU.max))
                link(nc.vector.tensor_tensor(t8b[:], left[:], per_expert(t1[:]), ALU.is_equal))
                link(nc.vector.tensor_tensor(t8b[:], t8b[:], per_tile(e_f[:]), ALU.mult))
                link(nc.vector.tensor_reduce(t1[:], t8b[:], AX.X, ALU.min))
                link(nc.vector.tensor_tensor(oh[k][:], per_tile(e_f[:]), per_expert(t1[:]), ALU.is_equal))
                if k == 0:
                    link(nc.vector.scalar_tensor_tensor(out=t8a[:], in0=oh[0][:], scalar=-2.0, in1=gate_probs[:], op0=ALU.mult, op1=ALU.add))
                    left = t8a
            link(nc.vector.tensor_tensor(t8b[:], oh[0][:], oh[1][:], ALU.add))
            link(nc.vector.tensor_copy(chosen16[:], t8b[:]))
            nc.vector.scalar_tensor_tensor(out=rows[:, :, GATE_COL:GATE_COL + EXPERTS], in0=t8b[:], scalar=W_SCALE ** -2,
                                           in1=gate_probs[:], op0=ALU.mult, op1=ALU.mult).then_inc(gates_ready, 1)
            dve.wait_ge(ff_bias_in, 48)
            nc.vector.tensor_scalar(b3_sb[:], b3_sb[:], W_SCALE, None, ALU.mult)
            link(nc.vector.tensor_scalar(b2_all[:, 0:EXPERTS, :], b2_all[:, 0:EXPERTS, :], W_SCALE ** 2, None, ALU.mult))
            dve.wait_ge(ranked, 1)
            link(nc.vector.tensor_copy(cnt[0][:], ps[:, 2, 0:ALL_TILES * EXPERTS].rearrange("p (t e) -> p t e", e=EXPERTS)))
            src, step_ = 0, 1
            while step_ < ALL_TILES:
                nc.vector.tensor_copy(cnt[1 - src][:, 0:step_, :], cnt[src][:, 0:step_, :])
                link(nc.vector.tensor_tensor(cnt[1 - src][:, step_:, :], cnt[src][:, step_:, :], cnt[src][:, 0:ALL_TILES - step_, :], ALU.add))
                src, step_ = 1 - src, 2 * step_
            totals = cnt[src][:, ALL_TILES - 1, :]
            link(nc.vector.tensor_tensor(nb_cmp[:], totals.unsqueeze(2).broadcast_to([P, EXPERTS, LIST_BLOCKS]),
                                         s_f[:].unsqueeze(1).broadcast_to([P, EXPERTS, LIST_BLOCKS]), ALU.is_gt))
            link(nc.vector.tensor_reduce(nb[0][:], nb_cmp[:], AX.X, ALU.add))
            link(nc.vector.tensor_copy(nb[2][:], nb[0][:]))
            at, d = 0, 1
            while d < EXPERTS:
                nc.vector.tensor_copy(nb[1 - at][:, 0:d], nb[at][:, 0:d])
                link(nc.vector.tensor_tensor(nb[1 - at][:, d:], nb[at][:, d:], nb[at][:, 0:EXPERTS - d], ALU.add))
                at, d = 1 - at, 2 * d
            ends = nb[at]
            link(nc.vector.tensor_tensor(list_at[:], ends[:], nb[2][:], ALU.subtract))
            link(nc.vector.tensor_scalar(list_at[:], list_at[:], float(GROUP), None, ALU.mult))
            link(nc.vector.tensor_tensor(t8a[:], cnt[src][:], ps[:, 1, 0:ALL_TILES * EXPERTS].rearrange("p (t e) -> p t e", e=EXPERTS), ALU.add))
            link(nc.vector.tensor_tensor(cnt[1 - src][:], per_tile(list_at[:]),
                                         ps[:, 2, 0:ALL_TILES * EXPERTS].rearrange("p (t e) -> p t e", e=EXPERTS), ALU.subtract))
            link(nc.vector.tensor_tensor(t8a[:], t8a[:], cnt[1 - src][:], ALU.add))
            for k in range(TOP_K):
                link(nc.vector.tensor_tensor(t8b[:], t8a[:], oh[k][:], ALU.mult))
                link(nc.vector.tensor_reduce(slot_f[:, k, :], t8b[:], AX.X, ALU.add))
            nc.vector.tensor_copy(slot[:], slot_f[:]).then_inc(ids_ready, 1)
            link(nc.vector.tensor_tensor(blk_cmp[:], blk_f[:].unsqueeze(2).broadcast_to([1, BLOCKS, EXPERTS - 1]),
                                         ends[0:1, 0:EXPERTS - 1].unsqueeze(1).broadcast_to([1, BLOCKS, EXPERTS - 1]), ALU.is_ge))
            link(nc.vector.tensor_reduce(blk_f[:], blk_cmp[:], AX.X, ALU.add))
            nc.vector.tensor_copy(blk_e[:], blk_f[:]).then_inc(ids_ready, 1)
            def ff_step(shared, first):
                def step(i, known):
                    a = i + -1
                    if exists(a, known):
                        n = first + a.n
                        e = EXPERTS if shared else dve.value_load(blk_e[0:1, bass.ds(a.n, 1)], min_val=0, max_val=EXPERTS - 1)
                        dve.wait_ge(sil_made, n + 1)
                        dve.wait_ge(b_made, n + 1)
                        need(dve, h_hi_made, n - 1)
                        for m in range(CHUNKS):
                            last = nc.vector.scalar_tensor_tensor(out=h_f[a.k % 2][:, m, :], in0=ps[:, 4 + a.k % 2, GROUP * m:GROUP * m + GROUP],
                                                                  scalar=b3_sb[:, e, m:m + 1], in1=sil[a.k % 2][:, m, :], op0=ALU.add, op1=ALU.mult)
                        last.then_inc(h_made, 1)
                    t = i + 1
                    if exists(t, known):
                        split_x(t, first)
                    if exists(a, known):
                        n = first + a.n
                        dve.wait_ge(h_hi_made, n + 1)
                        nc.vector.tensor_tensor(h_lo[a.k % 2][:], h_f[a.k % 2][:], h_hi[a.k % 2][:], ALU.subtract).then_inc(h_lo_made, 1)
                    y = i + -2
                    if shared:
                        if exists(y, known):
                            n = first + y.n
                            dve.wait_ge(y_made, n + 1)
                            if isinstance(y.n, int) and y.n == 0:
                                dve.wait_ge(shared_bias_in_x, 2 * BATCH)
                            tiles = X[:, bass.ds(2 * y.n, 2), :]
                            nc.vector.scalar_tensor_tensor(out=tiles, in0=ps[:, 6 + y.k % 2, :].rearrange("p (t d) -> p t d", t=2), scalar=W_SCALE ** -2,
                                                           in1=tiles, op0=ALU.mult, op1=ALU.add).then_inc(y_read, 1)
                    else:
                        if exists(y, known):
                            e = dve.value_load(blk_e[0:1, bass.ds(y.n, 1)], min_val=0, max_val=EXPERTS - 1)
                            dve.wait_ge(y_read, first + y.n + 1)
                            for t_ in range(2):
                                last = nc.vector.scalar_tensor_tensor(out=y_sb[y.k % 2][:, t_, :], in0=b2_all[:, e, :],
                                                                      scalar=blk_rows[y.k][:, t_, bass.ds(GATE_COL + e, 1)],
                                                                      in1=y_sb[y.k % 2][:, t_, :], op0=ALU.mult, op1=ALU.add)
                            last.then_inc(y_ready, 1)
                return step

            def split_x(t, first):
                n = first + t.n
                dve.wait_ge(x_hi_made, n + 1)
                nc.vector.tensor_tensor(x_lo[t.k % 2][:].rearrange("p c t -> p (c t)"), ps[:, t.k % 2, :],
                                        x_hi[t.k % 2][:].rearrange("p c t -> p (c t)"), ALU.subtract).then_inc(x_lo_made, 1)

            split_x(Block(0, 0), 0)
            each_block(dve, ff_step(True, 0), SHARED_BLOCKS)
            split_x(Block(0, 0), SHARED_BLOCKS)
            each_block(dve, ff_step(False, SHARED_BLOCKS), BLOCKS)

        @block.scalar
        def _(act):
            act.wait_ge(w_in, 96)

            def copy_xT(b, s):
                n = 2 * b + s
                act.wait_ge(turned[s], b + 1)
                act.wait_ge(v_made[s], 2 * b)
                for c in range(CHUNKS):
                    last = nc.scalar.copy(xnT[s][:, c, :], ps[:, 6 + c, :])
                last.then_inc(xT_copied, 1)

            def keep_hi(b, s):
                n = 2 * b + s
                act.wait_ge(qk_stored[s], 32 * b)
                for i in range(4):
                    act.wait_ge(qk_made, 4 * n + i + 1)
                    nc.scalar.activation(qk_hi[s][:, i, :], ps[:, i, :], ACT.Identity,
                                         bias=qk_bias[:, i:i + 1]).then_inc(hi_made, 1)

            halves(act, copy_xT, keep_hi)

            def copy_out(b, hf, g):
                G = 4 * b + 2 * hf + g
                act.wait_ge(pv_done[2], UNIT_STEPS // 3 * (2 * b + hf) + (STEPS // 3) * (g + 1))
                nc.scalar.copy(oT[:], PO).then_inc(ot_full, 1)

            def unit(b, hf, ahead, prior):
                R = 2 * b + hf
                for q in range(UNIT_STEPS):
                    width = 512 if q % STEPS < 2 else 320
                    for p in range(2):
                        act.wait_ge(st_full[p], UNIT_STEPS * R + q + 1)
                        if p == 0:
                            act.wait_ge(pv_done[q % 3], UNIT_STEPS // 3 * R + q // 3)
                        nc.scalar.activation(probs[q % 3][:, 2 * p:2 * p + 2, 0:width], ST[p][:, :, 0:width],
                                             ACT.Exp, scale=SCALE).then_inc(exped[p], 1)
                    if q == 0 and prior:
                        copy_out(*prior, 1)
                    if q == STEPS:
                        copy_out(b, hf, 0)
                if not ahead:
                    copy_out(b, hf, 1)

            def first():
                act.wait_ge(xw_in, 128)
                for m in range(CHUNKS):
                    act.wait_ge(kc_made, m + 1)
                    nc.scalar.activation(KcT[:, m, :], ps[:, m, 0:BATCH * KEYS], ACT.Identity, bias=xb_sb[:, CHUNKS + m:CHUNKS + m + 1]).then_inc(kc_kept, 1)
                act.wait_ge(gv_made, 3)
                for m in range(CHUNKS):
                    nc.scalar.copy(G[:, m, :], ps[:, 2 + m, 0:BATCH * KEYS])
                nc.scalar.copy(g0[:], ps[0:1, 0, 0:BATCH * KEYS]).then_inc(gv_kept, 1)

            rounds(act, first, unit)

            for j in range(2):
                act.wait_ge(att_free[j], 4 * BATCH)

            def copy_xT(n, s, turned, base, dst, free, ready):
                act.wait_ge(turned, n + 1)
                for sm, v in free:
                    act.wait_ge(sm, v)
                for c in range(CHUNKS):
                    last = nc.scalar.copy(dst[:, c, :], ps[:, base + c, :])
                last.then_inc(ready, 1)

            def split_weights(n, s, times):
                act.wait_ge(raw_in[s], 16 * times)
                flat = w_raw[s][:].rearrange("p a c d -> p (a c d)")
                nc.scalar.mul(w_hi[:, n, :, :, :].rearrange("p a c d -> p (a c d)"), flat, W_SCALE)
                nc.scalar.mul(flat, flat, W_SCALE).then_inc(scaled, 1)

            copy_xT(0, 0, turned2, 1, xT2[0], [], xT2_copied)

            def step(b, s, inner=False):
                n = halves_at(b, s)
                first, last = not inner and s == 0, not inner and s == 1
                act.wait_ge(neg_ready, n + 1)
                for t in range(HALF):
                    lastp = nc.scalar.activation(cp[:, t, 0:KEYS], ps[:, 0, KEYS * t:KEYS * t + KEYS], ACT.Exp, bias=neg_max[:, t:t + 1],
                                                 accum_out=row_sum[:, t:t + 1])
                lastp.then_inc(cp_ready, 1)
                act.wait_ge(cp_turned, n + 1)
                nc.scalar.copy(cpT[:], ps[:, 3, :]).then_inc(cpT_copied, 1)
                if not first:
                    copy_xT(n - 1, 1 - s, turned3, 6, xT3, [], xT3_copied)
                if not last:
                    copy_xT(n + 1, 1 - s, turned2, 1, xT2[1 - s], [], xT2_copied)
                split_weights(n, s, b + 1)

            each_half(act, step)
            copy_xT(2 * BATCH - 1, 1, turned3, 6, xT3, [], xT3_copied)
            split_weights(EXPERTS, 0, EXPERTS // 2 + 1)
            act.wait_ge(route, 2)
            nc.scalar.activation(gate_probs[:], logits[:], ACT.Exp).then_inc(exp_done, 1)
            act.wait_ge(ff_bias_in, 48)

            def high_x(t, first):
                n = first + t.n
                act.wait_ge(x_turned, n + 1)
                need(act, b_made, n - 1)
                nc.scalar.copy(x_hi[t.k % 2][:].rearrange("p c t -> p (c t)"), ps[:, t.k % 2, :]).then_inc(x_hi_made, 1)

            def ff_step(shared, first):
                def step(i, known):
                    a = i + -1
                    if exists(a, known):
                        n = first + a.n
                        e = EXPERTS if shared else act.value_load(blk_e[0:1, bass.ds(a.n, 1)], min_val=0, max_val=EXPERTS - 1)
                        act.wait_ge(a_made, n + 1)
                        need(act, h_made, n - 1)
                        for m in range(CHUNKS):
                            last = nc.scalar.activation(sil[a.k % 2][:, m, :], ps[:, 2 + a.k % 2, GROUP * m:GROUP * m + GROUP], ACT.Silu,
                                                        bias=b1_sb[:, e, m:m + 1], scale=1.0 / W_SCALE)
                        last.then_inc(sil_made, 1)
                    t = i + 1
                    if exists(t, known):
                        high_x(t, first)
                    if exists(a, known):
                        n = first + a.n
                        act.wait_ge(h_made, n + 1)
                        need(act, y_made, n - 1)
                        nc.scalar.copy(h_hi[a.k % 2][:], h_f[a.k % 2][:]).then_inc(h_hi_made, 1)
                    y = i + -2
                    if not shared and exists(y, known):
                        e = act.value_load(blk_e[0:1, bass.ds(y.n, 1)], min_val=0, max_val=EXPERTS - 1)
                        act.wait_ge(y_made, first + y.n + 1)
                        prior = y + -2
                        need(act, scattered[prior.k], 32 * (prior.quad + 1))
                        for t_ in range(2):
                            last = nc.scalar.activation(y_sb[y.k % 2][:, t_, :], ps[:, 6 + y.k % 2, DIM * t_:DIM * t_ + DIM], ACT.Copy,
                                                        scale=blk_rows[y.k][:, t_, bass.ds(GATE_COL + e, 1)])
                        last.then_inc(y_read, 1)
                return step

            high_x(Block(0, 0), 0)
            each_block(act, ff_step(True, 0), SHARED_BLOCKS)
            act.wait_ge(ids_ready, 2)
            high_x(Block(0, 0), SHARED_BLOCKS)
            each_block(act, ff_step(False, SHARED_BLOCKS), BLOCKS)

        @block.tensor
        def _(pe):
            pe.wait_ge(consts, 3)
            pe.wait_ge(w_in, 96)

            def turn(b, s):
                n = 2 * b + s
                pe.wait_ge(xn_ready, n + 1)
                pe.wait_ge(xT_copied, n)
                for c in range(CHUNKS):
                    for t in range(HALF):
                        last = nc.tensor.transpose(ps[:, 6 + c, P * t:P * t + P], xn[s][:, t, P * c:P * c + P], ident[:])
                last.then_inc(turned[s], 1)

            def project(b, s):
                n = 2 * b + s
                pe.wait_ge(xT_copied, n + 1)
                pe.wait_ge(qk_split, 4 * n)
                for i in range(4):
                    for c in range(CHUNKS):
                        last = nc.tensor.matmul(ps[:, i, :], w_sb[i // 2][:, c, P * (i % 2):P * (i % 2) + P], xnT[s][:, c, :],
                                                start=(c == 0), stop=(c == CHUNKS - 1))
                    last.then_inc(qk_made, 1)
                pe.wait_ge(v_kept, 2 * n)
                for t in range(HALF):
                    for c in range(CHUNKS):
                        last = nc.tensor.matmul(ps[:, 4 + t // 2, 256 * (t % 2):256 * (t % 2) + 256],
                                                xnT[s][:, c, P * t:P * t + P], w_sb[2][:, c, :],
                                                start=(c == 0), stop=(c == CHUNKS - 1))
                    if t % 2:
                        last.then_inc(v_made[s], 1)

            halves(pe, turn, project)
            pe.wait_ge(qk_split, 8 * BATCH)
            pe.wait_ge(v_kept, 4 * BATCH)
            pe.wait_ge(xT_copied, 2 * BATCH)

            def max_slot(uses, i, hf):
                h, j = divmod(i, STEPS)
                r = i % 2
                K, Q, W = Kst[hf][0:SHIFT_ROW, h, :], Qst[hf][0:SHIFT_ROW, h, :], WORK[r]
                pe.wait_ge(work_used[r], uses.next(r))
                if j < 2:
                    last = nc.tensor.matmul(W, Q[:, 0:P], K[:, 512 * j:512 * j + 512], start=True, stop=True)
                else:
                    t = j - 1
                    nc.tensor.matmul(W[:, 0:P], Q[:, P * t:P * t + P], K[:, 0:P], start=True, stop=True)
                    nc.tensor.matmul(W[0:64, P:320], Q[:, P * t:P * t + 64], K[:, P * t - 64:P * t + P], start=True, stop=True)
                    if t < TILES - 1:
                        last = nc.tensor.matmul(W[64:128, P:320], Q[:, P * t + 64:P * t + P], K[:, P * t:P * t + 192], start=True, stop=True)
                    else:
                        nc.tensor.matmul(W[64:128, P:256], Q[:, P * t + 64:P * t + P], K[:, P * t:P * t + P], start=True, stop=True)
                        last = nc.tensor.matmul(W[64:128, 256:320], Q[:, P * t + 64:P * t + P], K[:, P * t:P * t + 64], start=True, stop=True)
                last.then_inc(work_full[r], 1)

            def shift(uses, b, hf):
                pe.wait_ge(dve_step, 3 * (2 * b + hf) + 3)
                pe.wait_ge(work_used[0], uses.next(0))
                nc.tensor.transpose(WORK[0].bitcast(f16)[:, 0:P], mm[:], ident16[:]).then_inc(work_full[0], 1)

            def scores(b, hf, q, p):
                R = 2 * b + hf
                g, step = divmod(q, STEPS)
                pe.wait_ge(exped[p], UNIT_STEPS * R + q)
                for k in range(2):
                    h = 4 * g + 2 * p + k
                    K, Q, S = Kst[hf][:, h, :], Qst[hf][:, h, :], ST[p][:, k, :]
                    if step < 2:
                        last = nc.tensor.matmul(S, K[:, 0:P], Q[:, 512 * step:512 * step + 512], start=True, stop=True)
                    else:
                        t = step - 1
                        nc.tensor.matmul(S[:, 0:256].rearrange("p (a q) -> p a q", a=2), K[:, P * t:P * t + P],
                                         Q.rearrange("p (a q) -> p a q", q=P)[:, 0:t + 1:t, :], start=True, stop=True)
                        before = Q[:, P * t - 64:P * t]
                        after = Q[:, P * t + P:P * t + 192] if t < TILES - 1 else None
                        if t == 1:
                            last = nc.tensor.matmul(S[:, 256:320], K[:, P * t:P * t + P], after, start=True, stop=True)
                        elif t == TILES - 1:
                            last = nc.tensor.matmul(S[:, 256:320], K[:, P * t:P * t + P], before, start=True, stop=True)
                        else:
                            nc.tensor.matmul(S[0:64, 256:320], K[:, P * t:P * t + 64], before, start=True, stop=True)
                            last = nc.tensor.matmul(S[64:128, 256:320], K[:, P * t + 64:P * t + P], after, start=True, stop=True)
                last.then_inc(st_full[p], 1)

            def values(b, hf, q):
                R = 2 * b + hf
                g, step = divmod(q, STEPS)
                if q == 0:
                    pe.wait_ge(v_in[hf], 48 * (b + 1))
                if step == 0:
                    pe.wait_ge(ot_full, 2 * R + g)
                for p in range(2):
                    pe.wait_ge(exped[p], UNIT_STEPS * R + q + 1)
                pr = probs[q % 3]
                key_tile = max(step - 1, 0)

                def add(which, cols, tokens, start=False, stop=False):
                    for k in range(4):
                        bank, at = divmod(tokens.start, 512)
                        h = 4 * g + k
                        last = nc.tensor.matmul(PO[32 * k:32 * k + 32, bank, at:at + tokens.stop - tokens.start],
                                                V[hf][:, which, key_tile, h * VW:h * VW + 32],
                                                pr[:, k, cols], start=start, stop=stop, skip_group_check=True)
                    return last

                if step < 2:
                    for half in range(2):
                        last = add(0, slice(256 * half, 256 * half + 256), slice(512 * step + 256 * half, 512 * step + 256 * half + 256), start=half == 0)
                        if half == 0:
                            yield
                else:
                    t = key_tile
                    last = add(0, slice(0, P), slice(0, P), stop=t == TILES - 1)
                    last = add(0, slice(P, 2 * P), slice(P * t, P * t + P), stop=t == TILES - 1)
                    yield
                    if t > 1:
                        last = add(1, slice(256, 320), slice(P * t - 64, P * t), stop=t == TILES - 1)
                    if t < TILES - 1:
                        last = add(2, slice(256, 320), slice(P * t + P, P * t + 192))
                last.then_inc(pv_done[q % 3], 1)

            def turn_out(uses, b, hf, g, halves):
                G = 4 * b + 2 * hf + g
                pe.wait_ge(ot_full, G + 1)
                for j in halves:
                    pe.wait_ge(work_used[0], uses.next(0))
                    for t in range(HALF):
                        last = nc.tensor.transpose(WORK[0][:, P * t:P * t + P], oT[:, j, P * t:P * t + P], ident[:])
                    last.then_inc(work_full[0], 1)

            def keys_and_values():
                pe.wait_ge(xw_in, 128)
                for m in range(CHUNKS):
                    for c in range(CHUNKS):
                        last = nc.tensor.matmul(ps[:, m, 0:BATCH * KEYS], xw[1][:, c, P * m:P * m + P], ctx_sb[:, c, :], start=(c == 0), stop=(c == 1))
                    last.then_inc(kc_made, 1)
                    yield
                for b in range(BATCH):
                    for c in range(CHUNKS):
                        last = nc.tensor.matmul(ps[0:KEYS, 4 + b // 2, 256 * (b % 2):256 * (b % 2) + 256], ctx_sb[:, c, KEYS * b:KEYS * b + KEYS],
                                                xw[2][:, c, :], start=(c == 0), stop=(c == 1))
                    if b < BATCH - 1:
                        yield
                last.then_inc(gv_made, 1)
                yield
                pe.wait_ge(kc_kept, 2)
                for m in range(CHUNKS):
                    for c in range(CHUNKS):
                        last = nc.tensor.matmul(ps[:, 2 + m, 0:BATCH * KEYS], xw[0][:, c, P * m:P * m + P], KcT[:, c, :], start=(c == 0), stop=(c == 1))
                    if m < CHUNKS - 1:
                        yield
                last.then_inc(gv_made, 1)
                yield
                for c in range(CHUNKS):
                    last = nc.tensor.matmul(ps[0:1, 0, 0:BATCH * KEYS], xb_sb[:, c:c + 1], KcT[:, c, :], start=(c == 0), stop=(c == 1))
                last.then_inc(gv_made, 1)
                yield

            def first():
                uses = Uses([0, 0], ahead_of=1)
                others = keys_and_values()
                for i in range(MAX_SLOTS):
                    if i in (0, MAX_SLOTS // 2):
                        pe.wait_ge(stack_in[0][i > 0], 96)
                    max_slot(uses, i, 0)
                    if i % 4 == 3:
                        next(others, None)
                shift(uses, 0, 0)
                pe.wait_ge(gv_kept, 2)

            def unit(b, hf, ahead, prior):
                R = 2 * b + hf
                uses = Uses([R0_BEFORE + R0_ROUND * R, R1_MAX + R1_ROUND * R], ahead_of=1)
                if not prior:
                    uses.n[0] = 2
                pe.wait_ge(m_in[hf], 32 * (b + 1))
                for q in range(UNIT_STEPS + (0 if ahead else 1)):
                    slots = iter(range(TAKEN_BY[q], TAKEN_BY[q + 1]) if ahead else ())

                    def more(n=1):
                        for _, i in zip(range(n), slots):
                            if i in (0, MAX_SLOTS // 2):
                                pe.wait_ge(stack_in[ahead[1]][i > 0], 96 * (ahead[0] + 1))
                            max_slot(uses, i, ahead[1])

                    if q < UNIT_STEPS:
                        scores(b, hf, q, 0)
                    more()
                    if q < UNIT_STEPS:
                        scores(b, hf, q, 1)
                    more()
                    ending = (b, hf, q - 1) if q else (*prior, UNIT_STEPS - 1) if prior else None
                    if ending:
                        for _ in values(*ending):
                            more()
                    more(MAX_SLOTS)
                    if q - PRIOR_OUT_AT in (0, 1) and prior:
                        turn_out(uses, *prior, 1, [q - PRIOR_OUT_AT])
                    if q - OUT_AT in (0, 1):
                        turn_out(uses, b, hf, 0, [q - OUT_AT])
                    if q == SHIFT_AT and ahead:
                        shift(uses, *ahead)
                if not ahead:
                    turn_out(uses, b, hf, 1, range(2))

            rounds(pe, first, unit)

            for j in range(2):
                pe.wait_ge(att_free[j], 4 * BATCH)

            def turn(n, src, base, ready, copied, turned):
                pe.wait_ge(ready, n + 1)
                need(pe, copied, n)
                for c in range(CHUNKS):
                    for t in range(HALF):
                        last = nc.tensor.transpose(ps[:, base + c, P * t:P * t + P], src[:, t, P * c:P * c + P], ident[:])
                last.then_inc(turned, 1)

            def gates(n):
                pe.wait_ge(xT3_copied, n + 1)
                for t in range(HALF):
                    for c in range(CHUNKS):
                        last = nc.tensor.matmul(ps[:, 0, 320 + EXPERTS * t:320 + EXPERTS * t + EXPERTS], xT3[:, c, P * t:P * t + P], gate_sb[:, c, :],
                                                start=(c == 0), stop=(c == 1))
                last.then_inc(lg_made, 1)

            turn(0, xn2, 1, xn2_ready, xT2_copied, turned2)

            def step(b, s, inner=False):
                n = halves_at(b, s)
                first, last_ = not inner and s == 0, not inner and s == 1
                pe.wait_ge(xT2_copied, n + 1)
                if not first:
                    pe.wait_ge(lg_kept, n - 1) if not isinstance(n, int) else need(pe, lg_kept, n - 1)
                nc.tensor.matmul(ps[:, 0, 0:HALF * KEYS].rearrange("p (t k) -> p t k", k=KEYS), ones[:],
                                 g0[:, bass.ds(KEYS * b, KEYS)].unsqueeze(1).broadcast_to([1, HALF, KEYS]), start=True, stop=True)
                for t in range(HALF):
                    S = ps[:, 0, KEYS * t:KEYS * t + KEYS]
                    for c in range(CHUNKS):
                        last = nc.tensor.matmul(S, xT2[s][:, c, P * t:P * t + P], G[:, c, bass.ds(KEYS * b, KEYS)], start=False,
                                                stop=(c == CHUNKS - 1), skip_group_check=True)
                last.then_inc(cs_made, 1)
                if first:
                    pe.wait_ge(pads, 2)
                pe.wait_ge(cp_ready, n + 1)
                for t in range(HALF):
                    last = nc.tensor.transpose(ps[:, 3, P * t:P * t + P], cp[:, t, :], ident[:])
                last.then_inc(cp_turned, 1)
                if not first:
                    turn(n - 1, xn3[1 - s], 6, xn3_ready, xT3_copied, turned3)
                pe.wait_ge(cpT_copied, n + 1)
                for t in range(HALF):
                    last = nc.tensor.matmul(ps[:, 4 + t // 2, 256 * (t % 2):256 * (t % 2) + 256], cpT[:, P * t:P * t + P], Vc[:, b, :], start=True, stop=True)
                last.then_inc(cv_made, 1)
                if not last_:
                    turn(n + 1, xn2, 1, xn2_ready, xT2_copied, turned2)
                if not first:
                    gates(n - 1)

            each_half(pe, step)
            pe.wait_ge(lg_kept, 2 * BATCH - 1)
            turn(2 * BATCH - 1, xn3[1], 6, xn3_ready, xT3_copied, turned3)
            gates(2 * BATCH - 1)
            pe.wait_ge(gates_ready, 1)
            nc.tensor.matmul(ps[:, 1, 0:ALL_TILES * EXPERTS], before[:], chosen16[:].rearrange("p t e -> p (t e)"), start=True, stop=True)
            nc.tensor.matmul(ps[:, 2, 0:ALL_TILES * EXPERTS], every[:], chosen16[:].rearrange("p t e -> p (t e)"), start=True, stop=True).then_inc(ranked, 1)
            pe.wait_ge(low_made, EXPERTS + 1)
            pe.wait_ge(ids_ready, 1)

            PARTS = ((w_hi, 0), (w_lo, 0), (w_hi, 1))

            def turn_x(t, first):
                n = first + t.n
                pe.wait_ge(rows_in[t.k], 16 * (first // BUFS + t.quad + 1))
                need(pe, x_lo_made, n - 1)
                for c in range(CHUNKS):
                    for j in range(2):
                        last = nc.tensor.transpose(ps[:, t.k % 2, GROUP * c + P * j:GROUP * c + P * j + P], blk_rows[t.k][:, j, P * c:P * c + P], ident[:])
                last.then_inc(x_turned, 1)

            def ff_step(shared, first):
                def expert(of):
                    return EXPERTS if shared else pe.value_load(blk_e[0:1, bass.ds(of.n, 1)], min_val=0, max_val=EXPERTS - 1)

                def step(i, known):
                    if exists(i + 1, known):
                        turn_x(i + 1, first)
                    if exists(i, known):
                        n, r = first + i.n, i.k % 2
                        e = expert(i)
                        pe.wait_ge(x_hi_made, n + 1)
                        pe.wait_ge(x_lo_made, n + 1)
                        need(pe, h_made, n - 1)
                        for which, base, done in ((0, 2, a_made), (1, 4, b_made)):
                            for m in range(CHUNKS):
                                for c in range(CHUNKS):
                                    for j, (w, lo) in enumerate(PARTS):
                                        last = nc.tensor.matmul(ps[:, base + r, GROUP * m:GROUP * m + GROUP], w[:, e, which, c, P * m:P * m + P],
                                                                (x_lo if lo else x_hi)[r][:, c, :], start=(c == 0 and j == 0), stop=(c == 1 and j == 2))
                            last.then_inc(done, 1)
                    a = i + -1
                    if exists(a, known):
                        n, r = first + a.n, a.k % 2
                        e = expert(a)
                        pe.wait_ge(h_hi_made, n + 1)
                        pe.wait_ge(h_lo_made, n + 1)
                        need(pe, y_read, n - 1)
                        for t in range(2):
                            for c in range(CHUNKS):
                                for j, (w, lo) in enumerate(PARTS):
                                    last = nc.tensor.matmul(ps[:, 6 + r, DIM * t:DIM * t + DIM], (h_lo if lo else h_hi)[r][:, c, P * t:P * t + P],
                                                            w[:, e, 2, c, :], start=(c == 0 and j == 0), stop=(c == 1 and j == 2))
                        last.then_inc(y_made, 1)
                return step

            turn_x(Block(0, 0), 0)
            each_block(pe, ff_step(True, 0), SHARED_BLOCKS)
            pe.wait_ge(ids_ready, 2)
            turn_x(Block(0, 0), SHARED_BLOCKS)
            each_block(pe, ff_step(False, SHARED_BLOCKS), BLOCKS)



def kernel(**inputs):
    import numpy as _np
    import concourse.bacc as _bacc
    from concourse import mybir as _mybir
    from concourse.bass_utils import run_bass_kernel_spmd as _run

    nc = _bacc.Bacc("TRN2", target_bir_lowering=False, num_devices=1)
    f = lambda n: inputs["L0_ffn_" + n]
    up, gate, down = (_np.concatenate([f(n), f("s" + n)[None]]) for n in ("w1", "w3", "w2"))
    cols = lambda n: _np.concatenate([f(n), f("s" + n)[None]]).reshape(EXPERTS + 1, CHUNKS, P).transpose(2, 0, 1).reshape(P, -1)
    laid = dict(x=inputs["x"].reshape(BATCH * TOKENS, DIM),
                wq=inputs["L0_attn_Wq"].T, wk=inputs["L0_attn_Wk"].T, wv=inputs["L0_attn_Wv"].T,
                bq=inputs["L0_attn_bq"], bk=inputs["L0_attn_bk"], bv=inputs["L0_attn_bv"],
                ctxT=inputs["ctx_1024"].reshape(BATCH * KEYS, DIM).T,
                xwqT=inputs["L0_xattn_Wq"].T, xwk=inputs["L0_xattn_Wk"], xwv=inputs["L0_xattn_Wv"],
                xbq=inputs["L0_xattn_bq"], xbk=inputs["L0_xattn_bk"], xbv=inputs["L0_xattn_bv"],
                gateT=f("gate_w").T, w_all=_np.stack([up, gate, down], 1).reshape(EXPERTS + 1, 3 * DIM, DIM),
                b1=cols("b1"), b3=cols("b3"), b2=_np.concatenate([f("b2"), f("sb2")[None]]))
    arrays = {k: _np.ascontiguousarray(v) for k, v in laid.items()}
    args = [nc.dram_tensor("in_" + k, a.shape, _mybir.dt.from_np(a.dtype), kind="ExternalInput").ap() for k, a in arrays.items()]
    out = nc.dram_tensor("y", (BATCH * TOKENS, DIM), _mybir.dt.float32, kind="ExternalOutput").ap()
    program(nc, *args, out)
    r = _run(nc, [{"in_" + k: a for k, a in arrays.items()}], core_ids=[0])
    return _np.asarray(r.results[0]["y"]).reshape(BATCH, TOKENS, DIM)
```
